# Optimizing a Trainium2 kernel written in Bass

```python
import numpy as np
import jax
import jax.numpy as jnp

def _softmax(x, axis=-1):
    return jax.nn.softmax(x, axis=axis)

def _gelu(x):
    return jax.nn.gelu(x, approximate=True)

def _silu(x):
    return jax.nn.silu(x)

def _sigmoid(x):
    return jax.nn.sigmoid(x)

def _layernorm(x, axis=-1, eps=1e-05):
    m = jnp.mean(x, axis=axis, keepdims=True)
    v = jnp.var(x, axis=axis, keepdims=True)
    return (x - m) / jnp.sqrt(v + eps)

def _scatter_add(tgt, idx, src, axis=0):
    return tgt.at[idx].add(src)

def _segment_sum(src, seg, n):
    return jax.ops.segment_sum(src, seg, n)
kernel_name = 'mk_conv_preact_d2_conv_nhwc768_r4_aff2fd'

def setup_inputs(seed: int=0):
    np.random.seed(seed)
    _w = jnp.asarray

    def _rec_inputs():
        import jax
        import jax.numpy as jnp
        _gk = jax.random.key(seed)
        x = -0.0005963 + 1.001 * jax.random.normal(jax.random.fold_in(_gk, 1), (1, 16, 16, 192), jnp.float32)
        return x
    x = _rec_inputs()

    def _L0_conv_setup():
        import jax, jax.numpy as jnp
        import numpy as np
        B, H, W = (1, 16, 16)
        NUM_HEADS, KEY_DIM = (12, 16)
        C = NUM_HEADS * KEY_DIM

        def get_rel_pos(q_size, k_size, rel_pos):
            coords = jnp.arange(q_size)[:, None] - jnp.arange(k_size)[None, :] + (k_size - 1)
            return rel_pos[coords]
        key = jax.random.key(seed)
        ks = jax.random.split(key, 11)
        s = 0.02
        return {'x': jax.random.normal(ks[0], (B, H, W, C), jnp.float32), 'wq': jax.random.normal(ks[1], (C, C), jnp.float32) * s, 'bq': jnp.zeros((C,), jnp.float32), 'wk': jax.random.normal(ks[2], (C, C), jnp.float32) * s, 'bk': jnp.zeros((C,), jnp.float32), 'wv': jax.random.normal(ks[3], (C, C), jnp.float32) * s, 'bv': jnp.zeros((C,), jnp.float32), 'wo': jax.random.normal(ks[4], (C, C), jnp.float32) * s, 'bo': jnp.zeros((C,), jnp.float32), 'rel_pos_h': jax.random.normal(ks[5], (2 * H - 1, KEY_DIM), jnp.float32) * s, 'rel_pos_w': jax.random.normal(ks[6], (2 * W - 1, KEY_DIM), jnp.float32) * s}
    _L0_conv_all = _L0_conv_setup()
    _L0_conv_in = {k: v for k, v in _L0_conv_all.items() if k in ('wq', 'bq', 'wk', 'bk', 'wv', 'bv', 'wo', 'bo', 'rel_pos_h', 'rel_pos_w')}
    del _L0_conv_all

    def _L1_conv_setup():
        import jax, jax.numpy as jnp
        import numpy as np
        DIM = 192
        NUM_HEADS = 12
        HEAD_DIM = DIM // NUM_HEADS
        H = W = 16
        RANK = 4
        LORA_SCALING = 1.0 / RANK

        def _get_rel_pos(size, rel_pos):
            coords = jnp.arange(size)[:, None] - jnp.arange(size)[None, :] + (size - 1)
            return rel_pos[coords]
        key = jax.random.key(seed)
        ks = jax.random.split(key, 11)
        s = 0.02
        return {'x': jax.random.normal(ks[0], (1, H, W, DIM), dtype=jnp.float32), 'W_qkv': jax.random.normal(ks[1], (3 * DIM, DIM), dtype=jnp.float32) * s, 'b_qkv': jax.random.normal(ks[2], (3 * DIM,), dtype=jnp.float32) * s, 'A_q': jax.random.normal(ks[3], (RANK, DIM), dtype=jnp.float32) * s, 'B_q': jax.random.normal(ks[4], (DIM, RANK), dtype=jnp.float32) * s, 'A_v': jax.random.normal(ks[5], (RANK, DIM), dtype=jnp.float32) * s, 'B_v': jax.random.normal(ks[6], (DIM, RANK), dtype=jnp.float32) * s, 'rel_h': jax.random.normal(ks[7], (2 * H - 1, HEAD_DIM), dtype=jnp.float32) * s, 'rel_w': jax.random.normal(ks[8], (2 * W - 1, HEAD_DIM), dtype=jnp.float32) * s, 'W_proj': jax.random.normal(ks[9], (DIM, DIM), dtype=jnp.float32) * s, 'b_proj': jax.random.normal(ks[10], (DIM,), dtype=jnp.float32) * s}
    _L1_conv_all = _L1_conv_setup()
    _L1_conv_in = {k: v for k, v in _L1_conv_all.items() if k in ('W_qkv', 'b_qkv', 'A_q', 'B_q', 'A_v', 'B_v', 'rel_h', 'rel_w', 'W_proj', 'b_proj')}
    del _L1_conv_all
    return {'x': x, 'L0_conv_wq': _L0_conv_in['wq'], 'L0_conv_bq': _L0_conv_in['bq'], 'L0_conv_wk': _L0_conv_in['wk'], 'L0_conv_bk': _L0_conv_in['bk'], 'L0_conv_wv': _L0_conv_in['wv'], 'L0_conv_bv': _L0_conv_in['bv'], 'L0_conv_wo': _L0_conv_in['wo'], 'L0_conv_bo': _L0_conv_in['bo'], 'L0_conv_rel_pos_h': _L0_conv_in['rel_pos_h'], 'L0_conv_rel_pos_w': _L0_conv_in['rel_pos_w'], 'L1_conv_W_qkv': _L1_conv_in['W_qkv'], 'L1_conv_b_qkv': _L1_conv_in['b_qkv'], 'L1_conv_A_q': _L1_conv_in['A_q'], 'L1_conv_B_q': _L1_conv_in['B_q'], 'L1_conv_A_v': _L1_conv_in['A_v'], 'L1_conv_B_v': _L1_conv_in['B_v'], 'L1_conv_rel_h': _L1_conv_in['rel_h'], 'L1_conv_rel_w': _L1_conv_in['rel_w'], 'L1_conv_W_proj': _L1_conv_in['W_proj'], 'L1_conv_b_proj': _L1_conv_in['b_proj']}

def reference(x, L0_conv_wq, L0_conv_bq, L0_conv_wk, L0_conv_bk, L0_conv_wv, L0_conv_bv, L0_conv_wo, L0_conv_bo, L0_conv_rel_pos_h, L0_conv_rel_pos_w, L1_conv_W_qkv, L1_conv_b_qkv, L1_conv_A_q, L1_conv_B_q, L1_conv_A_v, L1_conv_B_v, L1_conv_rel_h, L1_conv_rel_w, L1_conv_W_proj, L1_conv_b_proj):
    import jax
    import jax.numpy as jnp

    def _L0_conv_ref(x, wq, bq, wk, bk, wv, bv, wo, bo, rel_pos_h, rel_pos_w):
        import jax, jax.numpy as jnp
        import numpy as np
        B, H, W = (1, 16, 16)
        NUM_HEADS, KEY_DIM = (12, 16)
        C = NUM_HEADS * KEY_DIM

        def get_rel_pos(q_size, k_size, rel_pos):
            coords = jnp.arange(q_size)[:, None] - jnp.arange(k_size)[None, :] + (k_size - 1)
            return rel_pos[coords]
        Bn, Hh, Ww, Cc = x.shape
        nh, kd = (NUM_HEADS, KEY_DIM)
        scale = kd ** 0.5

        def proj_heads(w, b):
            y = x @ w + b
            y = y.reshape(Bn, Hh * Ww, nh, kd).transpose(0, 2, 1, 3)
            return y.reshape(Bn * nh, Hh * Ww, kd)
        q = proj_heads(wq, bq)
        k = proj_heads(wk, bk)
        v = proj_heads(wv, bv)
        attn = jnp.einsum('bqd,bkd->bqk', q * scale, k)
        Rh = get_rel_pos(Hh, Hh, rel_pos_h)
        Rw = get_rel_pos(Ww, Ww, rel_pos_w)
        rq = q.reshape(Bn * nh, Hh, Ww, kd)
        rel_h = jnp.einsum('bhwc,hkc->bhwk', rq, Rh)
        rel_w = jnp.einsum('bhwc,wkc->bhwk', rq, Rw)
        attn = attn.reshape(Bn * nh, Hh, Ww, Hh, Ww) + rel_h[..., :, None] + rel_w[..., None, :]
        attn = jax.nn.softmax(attn.reshape(Bn * nh, Hh * Ww, Hh * Ww), axis=-1)
        out = attn @ v
        out = out.reshape(Bn, nh, Hh, Ww, kd).transpose(0, 2, 3, 1, 4).reshape(Bn, Hh, Ww, Cc)
        return out @ wo + bo

    def _L1_conv_ref(x, W_qkv, b_qkv, A_q, B_q, A_v, B_v, rel_h, rel_w, W_proj, b_proj):
        import jax, jax.numpy as jnp
        import numpy as np
        DIM = 192
        NUM_HEADS = 12
        HEAD_DIM = DIM // NUM_HEADS
        H = W = 16
        RANK = 4
        LORA_SCALING = 1.0 / RANK

        def _get_rel_pos(size, rel_pos):
            coords = jnp.arange(size)[:, None] - jnp.arange(size)[None, :] + (size - 1)
            return rel_pos[coords]
        B, h, w, dim = x.shape
        nh, hd = (NUM_HEADS, HEAD_DIM)
        scale = hd ** (-0.5)
        n = h * w
        xf = x.reshape(B, n, dim)
        qkv = xf @ W_qkv.T + b_qkv
        dq = xf @ A_q.T @ B_q.T * LORA_SCALING
        dv = xf @ A_v.T @ B_v.T * LORA_SCALING
        qkv = qkv.at[..., :dim].add(dq).at[..., 2 * dim:].add(dv)
        qkv = qkv.reshape(B, n, 3, nh, hd).transpose(2, 0, 3, 1, 4).reshape(3, B * nh, n, hd)
        q, k, v = (qkv[0], qkv[1], qkv[2])
        attn = q * scale @ jnp.swapaxes(k, -2, -1)
        Rh = _get_rel_pos(h, rel_h)
        Rw = _get_rel_pos(w, rel_w)
        r_q = q.reshape(B * nh, h, w, hd)
        bias_h = jnp.einsum('bhwc,hkc->bhwk', r_q, Rh)
        bias_w = jnp.einsum('bhwc,wkc->bhwk', r_q, Rw)
        attn = (attn.reshape(B * nh, h, w, h, w) + bias_h[:, :, :, :, None] + bias_w[:, :, :, None, :]).reshape(B * nh, n, n)
        attn = jax.nn.softmax(attn, axis=-1)
        out = (attn @ v).reshape(B, nh, h, w, hd).transpose(0, 2, 3, 1, 4).reshape(B, h, w, dim)
        return out @ W_proj.T + b_proj

    def _gn(v, G=32, eps=1e-05):
        B_, H_, W_, C_ = v.shape
        g = v.reshape(B_, H_, W_, G, C_ // G)
        m = jnp.mean(g, axis=(1, 2, 4), keepdims=True)
        s = jnp.var(g, axis=(1, 2, 4), keepdims=True)
        return ((g - m) / jnp.sqrt(s + eps)).reshape(v.shape)

    def _ln_c(v, eps=1e-06):
        m = jnp.mean(v, axis=-1, keepdims=True)
        s = jnp.var(v, axis=-1, keepdims=True)
        return (v - m) / jnp.sqrt(s + eps)

    def _ln_t(v, eps=1e-05):
        m = jnp.mean(v, axis=-1, keepdims=True)
        s = jnp.var(v, axis=-1, keepdims=True)
        return (v - m) / jnp.sqrt(s + eps)

    def _to_tokens(v):
        B_, H_, W_, C_ = v.shape
        return v.reshape(B_, H_ * W_, C_)

    def _from_tokens(t, like):
        return t.reshape(like.shape)
    x = x + _L0_conv_ref(_gn(x), L0_conv_wq, L0_conv_bq, L0_conv_wk, L0_conv_bk, L0_conv_wv, L0_conv_bv, L0_conv_wo, L0_conv_bo, L0_conv_rel_pos_h, L0_conv_rel_pos_w)
    x = x + _L1_conv_ref(_gn(x), L1_conv_W_qkv, L1_conv_b_qkv, L1_conv_A_q, L1_conv_B_q, L1_conv_A_v, L1_conv_B_v, L1_conv_rel_h, L1_conv_rel_w, L1_conv_W_proj, L1_conv_b_proj)
    return x

_drawn_inputs = setup_inputs


def setup_inputs(seed=0):
    import zlib

    import numpy as np

    out = dict(_drawn_inputs(seed))
    spreads = {'L0_conv_bq': (0.0, 0.8),
     'L0_conv_bk': (0.0, 0.8),
     'L0_conv_bv': (0.0, 0.297),
     'L0_conv_bo': (0.0, 0.1)}
    factors = {'L0_conv_wq': 4.806,
     'L0_conv_wk': 4.626,
     'L0_conv_wv': 4.274,
     'L0_conv_rel_pos_h': 8.0,
     'L0_conv_rel_pos_w': 8.0,
     'L1_conv_W_qkv': 6.584,
     'L1_conv_b_qkv': 8.0,
     'L1_conv_A_q': 8.0,
     'L1_conv_B_q': 8.0,
     'L1_conv_A_v': 8.0,
     'L1_conv_B_v': 8.0,
     'L1_conv_rel_h': 8.0,
     'L1_conv_rel_w': 8.0,
     'L1_conv_W_proj': 5.146,
     'L1_conv_b_proj': 2.79}
    for name, (base, spread) in spreads.items():
        noise = np.random.default_rng([zlib.crc32(name.encode()), seed]).standard_normal(out[name].shape)
        drawn = base * np.exp(spread * noise) if base else spread * noise
        out[name] = jnp.asarray(drawn.astype(out[name].dtype))
    for name, factor in factors.items():
        out[name] = (out[name] * factor).astype(out[name].dtype)
    return out
```

```python
from contextlib import ExitStack

import concourse.bass as bass
from concourse import mybir

F32 = mybir.dt.float32
F32R = mybir.dt.float32r
ALU = mybir.AluOpType
ACT = mybir.ActivationFunctionType
AX = mybir.AxisListType

LAYERS = 2
P = 128
HW = 16
T = HW * HW
TT = T // P
C = 192
CH = 96
NC = C // CH
NH = 12
D = C // NH
G4 = 4
NG = NH // G4
PAIRS = NH // 2
GROUP = C // 32
R = 2 * HW - 1
RANK = 4
EPS = 1e-5
SCALE = [float(D) ** 0.5, float(D) ** -0.5]
LORA_SCALE = 1.0 / RANK
VW = 32


def attention_layers(nc, x, wq, bq, wk, bk, wv, bv, wo, bo, rel_h0, rel_w0,
                     w_qkv, b_qkv, a_q, b_q, a_v, b_v, rel_h1, rel_w1, w_proj, b_proj, out):
    ctx = ExitStack()
    with ctx:
        def sb(name, shape, dt=F32):
            return ctx.enter_context(nc.sbuf_tensor(name, shape, dt))

        def sem(name):
            return ctx.enter_context(nc.semaphore(name))

        ident = sb("ident", [P, P])
        anti = sb("anti", [R, R])
        gavg = sb("gavg", [CH, CH])
        gdev = sb("gdev", [CH, CH])
        pow_exp = sb("pow_exp", [CH, NC])
        onehot = sb("onehot", [P, HW, HW])
        head_mask = sb("head_mask", [P, G4])
        pick_q = sb("pick_q", [P, G4, P], F32R)
        pick_k = sb("pick_k", [P, G4, 64], F32R)
        pick_rh = sb("pick_rh", [P, G4, P], F32R)
        pick_rl = sb("pick_rl", [P, G4, P], F32R)
        ones4_raw = sb("ones4_raw", [4, 2, P])
        ones4 = sb("ones4", [4, 2, P], F32R)
        wqk = [sb(f"wqk{l}", [CH + 1, NC, 2 * C]) for l in range(LAYERS)]
        wvv = [sb(f"wvv{l}", [CH + 1, NC, C]) for l in range(LAYERS)]
        wout = [sb(f"wout{l}", [P, 2, C]) for l in range(LAYERS)]
        bo_col = sb("bo_col", [CH, NC])
        bproj = sb("bproj", [P, C])
        wraw = sb("wraw", [CH, 6, C])
        wpraw = sb("wpraw", [CH, NC, C])
        lora_a = sb("lora_a", [RANK, 2, C])
        lora_b = sb("lora_b", [CH, 2, NC, RANK])
        lora_bt = sb("lora_bt", [RANK, 2, C])
        rel_raw = sb("rel_raw", [R, 4, D])
        rel_rep = sb("rel_rep", [R, 4, 8, D])
        rel_hi = sb("rel_hi", [P, LAYERS, 2 * R], F32R)
        rel_lo = sb("rel_lo", [P, LAYERS, 2 * R], F32R)
        table = [sb(f"table{l}", [P, 2, 2, R, G4], F32R) for l in range(LAYERS)]
        xin = sb("xin", [P, TT, C])
        xt = [sb(f"xt{l}", [CH, NC, T]) for l in range(LAYERS)]
        stats = sb("stats", [CH, LAYERS, NC, 6])
        mv = sb("mv", [CH, LAYERS, NC, 2])
        gmd = sb("gmd", [CH, LAYERS, 4])
        ev = sb("ev", [CH, LAYERS, NC])
        vare = sb("vare", [CH, LAYERS, NC])
        rstd = sb("rstd", [CH, LAYERS, NC])
        xn = sb("xn", [CH + 1, NC, T])
        zq = sb("zq", [P, NG, T], F32R)
        zk = sb("zk", [P, NG, T], F32R)
        va = sb("va", [P, TT, NH, VW])
        rr_hi = sb("rr_hi", [P, NG, T], F32R)
        rr_lo = sb("rr_lo", [P, NG, T], F32R)
        qs = sb("qs", [P, NH, T], F32R)
        ks = sb("ks", [P, NH, T], F32R)
        nm = sb("nm", [P, PAIRS, 4])
        nmhl = sb("nmhl", [P, PAIRS, TT, 2, 2], F32R)
        nmt = sb("nmt", [4, PAIRS, T], F32R)
        pt = sb("pt", [P, PAIRS, 2, TT, T])
        ot = sb("ot", [P, NG, T])
        rinv = sb("rinv", [P, NG, TT, G4])
        on = sb("on", [P, TT, C])
        ont = sb("ont", [P, 2, T])
        xres = sb("xres", [P, TT, C])
        res = sb("res", [P, TT, C])

        ps = ctx.enter_context(nc.psum_tensor("ps", [P, 8, 512], F32))

        ld_x, ld_wqk, ld_wv, ld_rel, ld_wo, ld_bo = (sem(n) for n in (
            "ld_x", "ld_wqk", "ld_wv", "ld_rel", "ld_wo", "ld_bo"))
        ld_qkv, ld_b1, ld_lora, ld_proj, ld_bproj, stored = (sem(n) for n in (
            "ld_qkv", "ld_b1", "ld_lora", "ld_proj", "ld_bproj", "stored"))
        zeroed, made_ident, made_anti, made_gavg, made_ones4, made_xones, made_va = (sem(n) for n in (
            "zeroed", "made_ident", "made_anti", "made_gavg", "made_ones4", "made_xones", "made_va"))
        made_gdev, made_mask, made_pick, made_rep = (sem(n) for n in (
            "made_gdev", "made_mask", "made_pick", "made_rep"))
        pick_zero, made_keys = sem("pick_zero"), sem("made_keys")
        (xt_ps, tab_ps, gn_ps, qk_ps, v_ps, rel_ps, ksel_ps, qsel_ps, s_ps, st_ps, nmt_ps, o_ps,
         oq_ps, ont_ps, y_ps, bt_ps, wt_ps, wpt_ps, xr_ps) = (sem(n) for n in (
            "xt_ps", "tab_ps", "gn_ps", "qk_ps", "v_ps", "rel_ps", "ksel_ps", "qsel_ps", "s_ps",
            "st_ps", "nmt_ps", "o_ps", "oq_ps", "ont_ps", "y_ps", "bt_ps", "wt_ps", "wpt_ps", "xr_ps"))
        (xt_sb, relhi_sb, z_hi, rr_hi_sb, ks_act, qs_act, nmt_sb, p_sb, ot_sb, ont_sb, bt_sb,
         wt_sb, wpt_sb) = (sem(n) for n in (
            "xt_sb", "relhi_sb", "z_hi", "rr_hi_sb", "ks_act", "qs_act", "nmt_sb", "p_sb", "ot_sb",
            "ont_sb", "bt_sb", "wt_sb", "wpt_sb"))
        (rello_sb, tab_sb, bn, gn, xn_sb, z_lo, v_sb, rr_lo_sb, ks_dve, qs_dve, max_sb, nm_hi,
         nm_lo, ri_sb, on_sb, x1_sb, xr_sb, res_sb) = (sem(n) for n in (
            "rello_sb", "tab_sb", "bn", "gn", "xn_sb", "z_lo", "v_sb", "rr_lo_sb", "ks_dve",
            "qs_dve", "max_sb", "nm_hi", "nm_lo", "ri_sb", "on_sb", "x1_sb", "xr_sb", "res_sb"))
        rstd_sb = sem("rstd_sb")

        GN_BANK = [4, 1]
        V_BANK = 3
        REL_BANK = 4
        K_BANK = [0, 1, 2, 3, 0, 1]
        Q_BANK = [2, 3, 4, 5, 6, 7]
        S_BANK = [0, 2]
        ST_BANK, O_BANK, NM_BANK = 4, 6, 7
        ONT_BANK = [7, 0]
        Y_BANK = 2
        ON_ROWS = [P, C - P]

        tokens = x.rearrange("b h w c -> (b h w) c").rearrange("(t p) c -> p t c", p=P)
        out_tokens = out.rearrange("b h w c -> (b h w) c").rearrange("(t p) c -> p t c", p=P)

        def row(v):
            return v.rearrange("(a n) -> a n", a=1)

        def chunks(w):
            return w.rearrange("(k p) n -> p k n", p=CH)

        block = ctx.enter_context(nc.Block())

        @block.sync
        def _(sp):
            sp.dma_start(xin[:, :, :], tokens).then_inc(ld_x, 16)
            sp.dma_start(wqk[0][0:CH, :, 0:C], chunks(wq)).then_inc(ld_wqk, 16)
            sp.dma_start(wqk[0][0:CH, :, C:2 * C], chunks(wk)).then_inc(ld_wqk, 16)
            sp.dma_start(wvv[0][0:CH, :, :], chunks(wv)).then_inc(ld_wv, 16)
            sp.dma_start(wqk[0][CH:CH + 1, 0, 0:C], row(bq)).then_inc(ld_wqk, 16)
            sp.dma_start(wqk[0][CH:CH + 1, 0, C:2 * C], row(bk)).then_inc(ld_wqk, 16)
            sp.dma_start(wvv[0][CH:CH + 1, 0, :], row(bv)).then_inc(ld_wv, 16)
            sp.dma_start(wraw[:, :, :], chunks(w_qkv)).then_inc(ld_qkv, 16)
            sp.dma_start(wpraw[:, :, :], chunks(w_proj)).then_inc(ld_proj, 16)
            sp.dma_start(wqk[1][CH:CH + 1, 0, :], row(b_qkv)[:, 0:2 * C]).then_inc(ld_b1, 16)
            sp.dma_start(wvv[1][CH:CH + 1, 0, :], row(b_qkv)[:, 2 * C:3 * C]).then_inc(ld_b1, 16)
            sp.dma_start(bproj[:, :], row(b_proj).to_broadcast([P, C])).then_inc(ld_bproj, 16)
            for s, (a, b) in enumerate(((a_q, b_q), (a_v, b_v))):
                sp.dma_start(lora_a[:, s, :], a).then_inc(ld_lora, 16)
                sp.dma_start(lora_b[:, s, :, :], chunks(b)).then_inc(ld_lora, 16)
            for t in range(TT):
                sp.wait_ge(res_sb, t + 1)
                sp.dma_start(out_tokens[:, t, :], res[:, t, :]).then_inc(stored, 16)
            sp.wait_ge(stored, 16 * TT)

        def rel_src(which, half):
            v = ps[0:64, REL_BANK + 2 * which + half, 0:8 * NG * HW]
            if which == 0:
                return v.rearrange("p (h g w) -> p g h w", g=NG, w=HW)
            return v.rearrange("p (w g h) -> p g h w", g=NG, h=HW)

        def rel_dst(tile, which, half):
            v = tile[64 * which:64 * which + 64, :, :].rearrange("p g (h w) -> p g h w", w=HW)
            return v[:, :, 8 * half:8 * half + 8, :] if which == 0 else v[:, :, :, 8 * half:8 * half + 8]

        def chunk_rows(which, g):
            m = 64 * (g + NG * which)
            return ps[m % P:m % P + 64, m // P, 0:T]

        @block.gpsimd
        def _(pool):
            pool.memset(ident[:, :], 0.0).then_inc(zeroed, 1)
            pool.wait_ge(zeroed, 1)
            pool.affine_select(out=ident[:, :], in_=ident[:, :], compare_op=ALU.not_equal, fill=1.0,
                               base=0, pattern=[[-1, P]], channel_multiplier=1).then_inc(made_ident, 1)
            pool.memset(gavg[:, :], 1.0 / GROUP).then_inc(zeroed, 1)
            pool.memset(anti[:, :], 0.0).then_inc(zeroed, 1)
            pool.wait_ge(zeroed, 3)
            pool.affine_select(out=anti[:, :], in_=anti[:, :], compare_op=ALU.not_equal, fill=1.0,
                               base=-(R - 1), pattern=[[1, R]], channel_multiplier=1).then_inc(made_anti, 1)
            gv = gavg[:, :].rearrange("p (g k) -> p g k", k=GROUP)
            pool.affine_select(out=gv, in_=gv, compare_op=ALU.is_ge, fill=0.0, base=0,
                               pattern=[[-GROUP, CH // GROUP], [0, GROUP]],
                               channel_multiplier=1).then_inc(zeroed, 1)
            pool.wait_ge(zeroed, 4)
            pool.affine_select(out=gv, in_=gv, compare_op=ALU.is_ge, fill=0.0, base=GROUP - 1,
                               pattern=[[GROUP, CH // GROUP], [0, GROUP]],
                               channel_multiplier=-1).then_inc(made_gavg, 1)
            pool.memset(pow_exp[:, :], -0.5).then_inc(zeroed, 1)
            pool.memset(onehot[:, :, :], 0.0).then_inc(zeroed, 1)
            for n, steps in enumerate(([-1, 0], [0, -1], [-1, 0], [0, -1])):
                pool.wait_ge(zeroed, 6 + n)
                pool.affine_select(out=onehot[:, :, :], in_=onehot[:, :, :], compare_op=ALU.not_equal,
                                   fill=1.0, base=-(64 + D * n), pattern=[[s_, HW] for s_ in steps],
                                   channel_multiplier=1).then_inc(zeroed, 1)
            pool.wait_ge(gn, 4)
            pool.tensor_tensor(rstd[:, 0, :], vare[:, 0, :], pow_exp[:, :], ALU.pow).then_inc(rstd_sb, 1)
            pool.memset(va[:, :, :, D:VW], 0.0).then_inc(zeroed, 1)
            pool.memset(ones4_raw[:, :, :], 1.0).then_inc(zeroed, 1)
            pool.wait_ge(zeroed, 12)
            pool.memset(va[:, :, :, D:D + 1], 1.0).then_inc(made_va, 1)
            pool.affine_select(out=ones4_raw[:, :, :], in_=ones4_raw[:, :, :],
                               compare_op=ALU.is_ge, fill=0.0, base=0, pattern=[[-2, 2], [0, P]],
                               channel_multiplier=1).then_inc(zeroed, 1)
            pool.wait_ge(zeroed, 13)
            pool.affine_select(out=ones4[:, :, :], in_=ones4_raw[:, :, :],
                               compare_op=ALU.is_ge, fill=0.0, base=1, pattern=[[2, 2], [0, P]],
                               channel_multiplier=-1).then_inc(made_ones4, 1)
            pool.wait_ge(gn, 8)
            pool.tensor_tensor(rstd[:, 1, :], vare[:, 1, :], pow_exp[:, :], ALU.pow).then_inc(rstd_sb, 1)

        @block.scalar
        def _(act):
            for n, rel in enumerate((rel_h0, rel_w0, rel_h1, rel_w1)):
                act.dma_start(rel_raw[:, n, :], rel).then_inc(ld_rel, 16)

            def copy(dst, src, scale=1.0):
                return act.activation(dst, src, ACT.Copy, scale=scale)

            act.wait_ge(xt_ps, 2)
            copy(xt[0][:, 1, :], ps[0:CH, 1, 0:T]).then_inc(xt_sb, 1)
            act.wait_ge(bn, 1)
            copy(xt[0][:, 0, :], ps[0:CH, 0, 0:T]).then_inc(xt_sb, 1)
            act.dma_start(wout[0][:, 0, :], wo[0:P, :]).then_inc(ld_wo, 16)
            act.dma_start(wout[0][0:C - P, 1, :], wo[P:C, :]).then_inc(ld_wo, 16)
            act.wait_ge(ld_rel, 64)
            for n in range(4):
                copy(rel_rep[:, n, :, :],
                     rel_raw[:, n, :].unsqueeze(1).to_broadcast([R, 8, D])).then_inc(made_rep, 1)
            act.wait_ge(made_ident, 1)
            by_head = ident[:, :].rearrange("p (s j c) -> p j s c", s=2, j=G4)
            by_pos = ident[:, :].rearrange("p (k j) -> p j k", j=G4)
            for n in range(2):
                copy(pick_k[:, :, :].rearrange("p j (s r c) -> p r j s c", s=2, r=2)[:, n],
                     by_head).then_inc(made_pick, 1)
            act.wait_ge(tab_ps, 1)
            for l in range(LAYERS):
                copy(rel_hi[:, l, :], ps[:, 2, l * 2 * R:(l + 1) * 2 * R],
                     scale=1.0 / SCALE[l]).then_inc(relhi_sb, 1)
            for n in range(2):
                copy(pick_q[:, :, 0:64].rearrange("p j (r s c) -> p r j s c", s=2, r=2)[:, n],
                     by_head).then_inc(made_pick, 1)
            copy(pick_rh[:, :, 64:96], by_pos).then_inc(made_pick, 1)
            copy(pick_rl[:, :, 96:128], by_pos).then_inc(made_pick, 1)
            act.wait_ge(zeroed, 10)
            copy(ks[64:P, :, :], onehot[64:P, :, :].rearrange("p a b -> p (a b)").unsqueeze(1)
                 .to_broadcast([64, NH, T])).then_inc(made_keys, 1)

            def key_tiles(l, p):
                act.wait_ge(ksel_ps, PAIRS * l + p + 1)
                copy(ks[0:64, 2 * p:2 * p + 2, :].rearrange("p a t -> p (a t)"),
                     ps[0:64, K_BANK[p], :]).then_inc(ks_act, 1)

            def out_columns(l, g):
                act.wait_ge(o_ps, NG * l + g + 1)
                copy(ot[:, g, :], ps[:, O_BANK, 0:T]).then_inc(ot_sb, 1)

            for l in range(LAYERS):
                if l == 1:
                    act.wait_ge(bt_ps, 1)
                    copy(lora_bt[:, :, :].rearrange("p a n -> p (a n)"), ps[0:RANK, 4, 0:2 * C],
                         scale=LORA_SCALE).then_inc(bt_sb, 1)
                    for ic in range(NC):
                        act.wait_ge(wt_ps, ic + 1)
                        copy(wqk[1][0:CH, ic, :], ps[0:CH, 5 + ic, 0:2 * C]).then_inc(wt_sb, 1)
                    act.wait_ge(wt_ps, 3)
                    copy(wvv[1][0:CH, :, :].rearrange("p k n -> p (k n)"),
                         ps[0:CH, 7, 0:2 * C]).then_inc(wt_sb, 1)
                    act.wait_ge(wpt_ps, 1)
                    copy(wout[1][:, 0, :], ps[:, 4, 0:C]).then_inc(wpt_sb, 1)
                    copy(wout[1][0:C - P, 1, :], ps[0:C - P, 4, C:2 * C]).then_inc(wpt_sb, 1)
                for which in range(2):
                    for g in range(NG):
                        act.wait_ge(qk_ps, 3 * l + (64 * (g + NG * which)) // P + 1)
                        copy((zq, zk)[which][0:64, g, :], chunk_rows(which, g)).then_inc(z_hi, 1)
                if l == 0:
                    act.dma_start(bo_col[:, :], bo.rearrange("(k p) -> p k", p=CH),
                                  allow_slow_non_contiguous=True).then_inc(ld_bo, 16)
                for which in range(2):
                    for half in range(2):
                        act.wait_ge(rel_ps, 4 * l + 2 * which + half + 1)
                        copy(rel_dst(rr_hi, which, half), rel_src(which, half)).then_inc(rr_hi_sb, 1)
                    if which == 0:
                        key_tiles(l, 0)
                        key_tiles(l, 2)
                    else:
                        key_tiles(l, 4)
                for p in (0, 2, 4):
                    act.wait_ge(qsel_ps, PAIRS * l + p + 1)
                    copy(qs[:, 2 * p:2 * p + 2, :].rearrange("p a t -> p (a t)"),
                         ps[:, Q_BANK[p], :]).then_inc(qs_act, 1)
                for p in range(PAIRS):
                    act.wait_ge(nmt_ps, PAIRS * l + p + 1)
                    copy(nmt[:, p, :], ps[0:4, NM_BANK, 0:T]).then_inc(nmt_sb, 1)
                    if p % 2 == 1 and p >= 3:
                        out_columns(l, (p - 3) // 2)
                    act.wait_ge(st_ps, PAIRS * l + p + 1)
                    act.activation(pt[:, p, :, :, :].rearrange("p a k t -> p a (k t)"),
                                   ps[:, ST_BANK:ST_BANK + 2, :], ACT.Exp,
                                   scale=SCALE[l]).then_inc(p_sb, 1)
                out_columns(l, NG - 1)
                for kc in range(2):
                    act.wait_ge(ont_ps, 2 * l + kc + 1)
                    copy(ont[0:ON_ROWS[kc], kc, :],
                         ps[0:ON_ROWS[kc], ONT_BANK[kc], 0:T]).then_inc(ont_sb, 1)

        @block.vector
        def _(dve):
            dve.memset(xn[CH:CH + 1, 0, :], 1.0).then_inc(made_xones, 1)
            dve.memset(pick_q[:, :, 64:P].bitcast(F32), 0.0).then_inc(pick_zero, 1)
            dve.memset(pick_rh[:, :, 0:64].bitcast(F32), 0.0).then_inc(pick_zero, 1)
            dve.memset(pick_rh[:, :, 96:P].bitcast(F32), 0.0).then_inc(pick_zero, 1)
            dve.memset(pick_rl[:, :, 0:96].bitcast(F32), 0.0).then_inc(pick_zero, 1)
            dve.wait_ge(made_ident, 1)
            dve.tensor_reduce(head_mask[:, :], ident[:, :].rearrange("p (s j c) -> p j s c", s=2, j=G4),
                              AX.XY, ALU.add).then_inc(made_mask, 1)
            dve.wait_ge(made_gavg, 1)
            dve.tensor_tensor(gdev[:, :], ident[0:CH, 0:CH], gavg[:, :], ALU.subtract).then_inc(made_gdev, 1)

            def key_tiles(l, p):
                dve.wait_ge(ksel_ps, PAIRS * l + p + 1)
                dve.tensor_copy(ks[0:64, 2 * p:2 * p + 2, :].rearrange("p a t -> p (a t)"),
                                ps[0:64, K_BANK[p], :]).then_inc(ks_dve, 1)

            def normalise(l, g):
                dve.wait_ge(oq_ps, NG * l + g + 1)
                q = ps[:, O_BANK, T:2 * T].rearrange("p (t j d) -> p t j d", t=TT, j=G4)
                dve.reciprocal(rinv[:, g, :, :], q[:, :, :, D]).then_inc(ri_sb, 1)
                dve.wait_ge(ri_sb, NG * l + g + 1)
                dve.tensor_tensor(
                    on[:, :, 64 * g:64 * g + 64].rearrange("p t (j d) -> p t j d", d=D), q[:, :, :, 0:D],
                    rinv[:, g, :, :].unsqueeze(3).to_broadcast([P, TT, G4, D]), ALU.mult).then_inc(on_sb, 1)

            for l in range(LAYERS):
                if l == 0:
                    dve.wait_ge(xt_ps, 1)
                    dve.bn_stats(stats[:, 0, 0, :], ps[0:CH, 0, 0:T]).then_inc(bn, 1)
                    dve.wait_ge(xt_sb, 1)
                    dve.bn_stats(stats[:, 0, 1, :], xt[0][:, 1, :]).then_inc(bn, 1)
                else:
                    for ic in range(NC):
                        dve.wait_ge(y_ps, ic + 1)
                        if ic == 0:
                            dve.wait_ge(ld_bo, 16)
                            dve.wait_ge(xt_sb, 2)
                        dve.scalar_tensor_tensor(out=xt[1][:, ic, :], in0=ps[0:CH, Y_BANK + ic, 0:T],
                                                 scalar=bo_col[:, ic:ic + 1], in1=xt[0][:, ic, :],
                                                 op0=ALU.add, op1=ALU.add).then_inc(x1_sb, 1)
                    for ic in range(NC):
                        dve.wait_ge(x1_sb, ic + 1)
                        dve.bn_stats(stats[:, 1, ic, :], xt[1][:, ic, :]).then_inc(bn, 1)
                for ic in range(NC):
                    dve.wait_ge(bn, 4 * l + ic + 1)
                    dve.bn_aggr(mv[:, l, ic, :], stats[:, l, ic, :]).then_inc(bn, 1)
                dve.wait_ge(gn_ps, 2 * l + 1)
                dve.tensor_copy(gmd[:, l, :], ps[0:CH, GN_BANK[l], 0:4]).then_inc(gn, 1)
                dve.wait_ge(gn, 4 * l + 1)
                for ic in range(NC):
                    dve.scalar_tensor_tensor(out=ev[:, l, ic:ic + 1], in0=gmd[:, l, 2 + ic:3 + ic],
                                             scalar=gmd[:, l, 2 + ic:3 + ic], in1=mv[:, l, ic, 1:2],
                                             op0=ALU.mult, op1=ALU.add).then_inc(gn, 1)
                dve.wait_ge(gn_ps, 2 * l + 2)
                dve.tensor_scalar(vare[:, l, :], ps[0:CH, GN_BANK[l], 4:6], EPS, None,
                                  ALU.add).then_inc(gn, 1)
                if l == 0:
                    dve.wait_ge(relhi_sb, LAYERS)
                    for k in range(LAYERS):
                        dve.scalar_tensor_tensor(out=rel_lo[:, k, :], in0=ps[:, 2, k * 2 * R:(k + 1) * 2 * R],
                                                 scalar=1.0 / SCALE[k], in1=rel_hi[:, k, :].bitcast(F32),
                                                 op0=ALU.mult, op1=ALU.subtract).then_inc(rello_sb, 1)
                dve.wait_ge(rstd_sb, l + 1)
                for ic in range(NC):
                    dve.tensor_scalar(xn[0:CH, ic, :], xt[l][:, ic, :], gmd[:, l, ic:ic + 1],
                                      rstd[:, l, ic:ic + 1], ALU.subtract, ALU.mult).then_inc(xn_sb, 1)
                if l == 0:
                    dve.wait_ge(made_mask, 1)
                    for k in range(LAYERS):
                        dve.wait_ge(rello_sb, k + 1)
                        for part, half in enumerate((rel_hi, rel_lo)):
                            dve.tensor_tensor(
                                table[k][:, part, :, :, :].rearrange("p s r j -> p (s r) j"),
                                half[:, k, :].bitcast(F32).unsqueeze(2).to_broadcast([P, 2 * R, G4]),
                                head_mask[:, :].unsqueeze(1).to_broadcast([P, 2 * R, G4]),
                                ALU.mult).then_inc(tab_sb, 1)
                for which in range(2):
                    for g in range(NG):
                        z = (zq, zk)[which]
                        dve.wait_ge(z_hi, 6 * l + NG * which + g + 1)
                        dve.tensor_tensor(z[64:P, g, :], chunk_rows(which, g), z[0:64, g, :].bitcast(F32),
                                          ALU.subtract).then_inc(z_lo, 1)
                dve.wait_ge(v_ps, l + 1)
                dve.tensor_copy(va[:, :, :, 0:D], ps[:, V_BANK, 0:TT * C].rearrange(
                    "p (t h d) -> p t h d", t=TT, d=D)).then_inc(v_sb, 1)
                if l == 1:
                    dve.wait_ge(ld_bproj, 16)
                    dve.wait_ge(xr_ps, 1)
                    dve.tensor_tensor(xres[:, :, :], ps[:, 6, 0:TT * C].rearrange("p (t n) -> p t n", t=TT),
                                      bproj[:, :].unsqueeze(1).to_broadcast([P, TT, C]),
                                      ALU.add).then_inc(xr_sb, 1)
                for which in range(2):
                    for half in range(2):
                        n = 4 * l + 2 * which + half + 1
                        dve.wait_ge(rr_hi_sb, n)
                        dve.tensor_tensor(rel_dst(rr_lo, which, half), rel_src(which, half),
                                          rel_dst(rr_hi, which, half).bitcast(F32),
                                          ALU.subtract).then_inc(rr_lo_sb, 1)
                    if which == 0:
                        key_tiles(l, 1)
                        key_tiles(l, 3)
                    else:
                        key_tiles(l, 5)
                for p in (1, 3, 5):
                    dve.wait_ge(qsel_ps, PAIRS * l + p + 1)
                    dve.tensor_copy(qs[:, 2 * p:2 * p + 2, :].rearrange("p a t -> p (a t)"),
                                    ps[:, Q_BANK[p], :]).then_inc(qs_dve, 1)
                for p in range(PAIRS):
                    n = PAIRS * l + p + 1
                    b = S_BANK[p % 2]
                    dve.wait_ge(s_ps, n)
                    dve.tensor_reduce(nm[:, p, :], ps[:, b:b + 2, :].rearrange("p a (t k) -> p (a t) k", k=T),
                                      AX.X, ALU.max, negate=True).then_inc(max_sb, 1)
                    by_tile = nm[:, p, :].rearrange("p (a t) -> p t a", t=TT)
                    dve.wait_ge(max_sb, n)
                    dve.tensor_copy(nmhl[:, p, :, :, 0], by_tile).then_inc(nm_hi, 1)
                    dve.wait_ge(nm_hi, n)
                    dve.tensor_tensor(nmhl[:, p, :, :, 1], by_tile, nmhl[:, p, :, :, 0].bitcast(F32),
                                      ALU.subtract).then_inc(nm_lo, 1)
                for g in range(NG):
                    normalise(l, g)
                if l == 1:
                    for t in range(TT):
                        dve.wait_ge(y_ps, NC + t + 1)
                        dve.tensor_tensor(res[:, t, :], ps[:, Y_BANK + t, 0:C], xres[:, t, :],
                                          ALU.add).then_inc(res_sb, 1)

        @block.tensor
        def _(pe):
            mm = pe.matmul
            pe.wait_ge(ld_x, 16)
            pe.wait_ge(made_ident, 1)
            for ic in range(NC):
                for t in range(TT):
                    last = pe.transpose(ps[0:CH, ic, t * P:(t + 1) * P], xin[:, t, ic * CH:(ic + 1) * CH],
                                        ident[:, :])
                last.then_inc(xt_ps, 1)
            pe.wait_ge(made_anti, 1)
            pe.wait_ge(made_rep, 4)
            for n in range(4):
                last = mm(ps[:, 2, n * R:(n + 1) * R], rel_rep[:, n, :, :].rearrange("r b c -> r (b c)"),
                          anti[:, :], start=True, stop=True)
            last.then_inc(tab_ps, 1)

            def group_means(l):
                pe.wait_ge(bn, 4 * l + 4)
                pe.wait_ge(made_gavg, 1)
                pe.wait_ge(made_gdev, 1)
                mm(ps[0:CH, GN_BANK[l], 0:2], gavg[:, :], mv[:, l, :, 0], start=True, stop=True)
                mm(ps[0:CH, GN_BANK[l], 2:4], gdev[:, :], mv[:, l, :, 0], start=True,
                   stop=True).then_inc(gn_ps, 1)

            def group_variance(l):
                pe.wait_ge(gn, 4 * l + 3)
                mm(ps[0:CH, GN_BANK[l], 4:6], gavg[:, :], ev[:, l, :], start=True,
                   stop=True).then_inc(gn_ps, 1)

            def turn(dst, src, first, last):
                return mm(dst, src, ident[0:CH, 0:CH], start=first, stop=last, is_transpose=True,
                          skip_group_check=True)

            def scores(l, p):
                if p == 0:
                    pe.wait_ge(made_keys, 1)
                    pe.wait_ge(ks_act, 3 * l + 3)
                    pe.wait_ge(ks_dve, 3 * l + 3)
                if p % 2 == 0:
                    pe.wait_ge(qs_act, 3 * l + p // 2 + 1)
                else:
                    pe.wait_ge(qs_dve, 3 * l + p // 2 + 1)
                if p >= 2:
                    pe.wait_ge(max_sb, PAIRS * l + p - 1)
                for a in range(2):
                    for t in range(TT):
                        last = mm(ps[:, S_BANK[p % 2] + a, t * T:(t + 1) * T],
                                  qs[:, 2 * p + a, t * P:(t + 1) * P], ks[:, 2 * p + a, :],
                                  start=True, stop=True)
                last.then_inc(s_ps, 1)

            def scores_t(l, p):
                if p == 0:
                    pe.wait_ge(qs_act, 3 * l + 2)
                    pe.wait_ge(qs_dve, 3 * l + 2)
                else:
                    pe.wait_ge(p_sb, PAIRS * l + p)
                for a in range(2):
                    for t in range(TT):
                        mm(ps[:, ST_BANK + a, t * T:(t + 1) * T], ks[:, 2 * p + a, t * P:(t + 1) * P],
                           qs[:, 2 * p + a, :], start=(t == 0), stop=False, skip_group_check=True)

            def turn_max(l, p):
                if p == 0:
                    pe.wait_ge(qs_dve, 3 * l + 3)
                pe.wait_ge(nm_lo, PAIRS * l + p + 1)
                for t in range(TT):
                    last = pe.transpose(ps[0:4, NM_BANK, t * P:(t + 1) * P],
                                        nmhl[:, p, t, :, :].bitcast(F32).rearrange("p a s -> p (a s)"),
                                        ident[:, :])
                last.then_inc(nmt_ps, 1)

            def add_max(l, p):
                if l == 0 and p == 0:
                    pe.wait_ge(made_ones4, 1)
                pe.wait_ge(nmt_sb, PAIRS * l + p + 1)
                for a in range(2):
                    for t in range(TT):
                        last = mm(ps[:, ST_BANK + a, t * T:(t + 1) * T], ones4[:, a, :], nmt[:, p, :],
                                  start=False, stop=True, skip_group_check=True)
                last.then_inc(st_ps, 1)

            def probs_v(l, g):
                if g == 0:
                    pe.wait_ge(qs_act, 3 * l + 3)
                    pe.wait_ge(v_sb, l + 1)
                    pe.wait_ge(made_va, 1)
                else:
                    pe.wait_ge(on_sb, NG * l + g)
                pe.wait_ge(p_sb, PAIRS * l + 2 * g + 2)
                for t in range(TT):
                    for j in range(G4):
                        last = mm(ps[32 * j:32 * j + 32, O_BANK, 0:T], va[:, t, G4 * g + j, :],
                                  pt[:, 2 * g + j // 2, j % 2, t, :], start=(t == 0), stop=(t == TT - 1))
                last.then_inc(o_ps, 1)

            def turn_out(l, g):
                pe.wait_ge(ot_sb, NG * l + g + 1)
                for t in range(TT):
                    last = pe.transpose(ps[:, O_BANK, T + t * P:T + (t + 1) * P],
                                        ot[:, g, t * P:(t + 1) * P], ident[:, :])
                last.then_inc(oq_ps, 1)

            def turn_on(l, kc):
                pe.wait_ge(on_sb, NG * l + 2 + kc)
                for t in range(TT):
                    last = pe.transpose(ps[0:ON_ROWS[kc], ONT_BANK[kc], t * P:(t + 1) * P],
                                        on[:, t, kc * P:kc * P + ON_ROWS[kc]], ident[:, :])
                last.then_inc(ont_ps, 1)

            for l in range(LAYERS):
                group_means(l)
                if l == 1:
                    pe.wait_ge(bt_sb, 1)
                    for ic in range(NC):
                        mm(ps[0:CH, 5 + ic, 0:C], lora_a[:, 0, ic * CH:(ic + 1) * CH], lora_bt[:, 0, :],
                           start=False, stop=True, skip_group_check=True).then_inc(wt_ps, 1)
                    for ic in range(NC):
                        last = mm(ps[0:CH, 7, ic * C:(ic + 1) * C], lora_a[:, 1, ic * CH:(ic + 1) * CH],
                                  lora_bt[:, 1, :], start=False, stop=True, skip_group_check=True)
                    last.then_inc(wt_ps, 1)
                group_variance(l)
                if l == 1:
                    pe.wait_ge(ld_proj, 16)
                    for b in range(NC):
                        pe.transpose(ps[:, 4, b * CH:(b + 1) * CH], wpraw[:, b, 0:P], ident[0:CH, 0:CH])
                        last = pe.transpose(ps[0:C - P, 4, C + b * CH:C + (b + 1) * CH], wpraw[:, b, P:C],
                                            ident[0:CH, 0:CH])
                    last.then_inc(wpt_ps, 1)
                pe.wait_ge(xn_sb, 2 * l + 2)
                if l == 0:
                    pe.wait_ge(made_xones, 1)
                    pe.wait_ge(ld_wqk, 64)
                else:
                    pe.wait_ge(ld_b1, 32)
                    pe.wait_ge(wt_sb, 2)
                for m in range(3):
                    mm(ps[:, m, 0:T], wqk[l][:, 0, m * P:(m + 1) * P], xn[:, 0, :], start=True, stop=False)
                    mm(ps[:, m, 0:T], wqk[l][0:CH, 1, m * P:(m + 1) * P], xn[0:CH, 1, :], start=False,
                       stop=True).then_inc(qk_ps, 1)
                if l == 0:
                    pe.wait_ge(ld_wv, 32)
                else:
                    pe.wait_ge(wt_sb, 3)
                for t in range(TT):
                    mm(ps[:, V_BANK, t * C:(t + 1) * C], xn[:, 0, t * P:(t + 1) * P], wvv[l][:, 0, :],
                       start=True, stop=False)
                    last = mm(ps[:, V_BANK, t * C:(t + 1) * C], xn[0:CH, 1, t * P:(t + 1) * P],
                              wvv[l][0:CH, 1, :], start=False, stop=True)
                last.then_inc(v_ps, 1)
                if l == 1:
                    for t in range(TT):
                        for ic in range(NC):
                            last = pe.transpose(ps[:, 6, t * C + ic * CH:t * C + (ic + 1) * CH],
                                                xt[1][:, ic, t * P:(t + 1) * P], ident[0:CH, 0:CH])
                    last.then_inc(xr_ps, 1)
                if l == 0:
                    pe.wait_ge(tab_sb, 4)
                else:
                    pe.wait_ge(wpt_sb, 2)
                pe.wait_ge(z_lo, 6 * l + NG)
                for which in range(2):
                    if which == 1 and l == 1:
                        pe.wait_ge(xr_sb, 1)
                    for i in range(HW):
                        if which == 0:
                            moving = zq[:, :, i * HW:(i + 1) * HW]
                        else:
                            moving = zq[:, :, :].rearrange("p g (h w) -> p g h w", w=HW)[:, :, :, i]
                        b, c = REL_BANK + 2 * which + i // 8, (i % 8) * NG * HW
                        for part in range(2):
                            last = mm(ps[0:64, b, c:c + NG * HW],
                                      table[l][:, part, which, HW - 1 - i:2 * HW - 1 - i, :].rearrange(
                                          "p r j -> p (r j)"), moving, start=(part == 0), stop=(part == 1))
                        if i % 8 == 7:
                            last.then_inc(rel_ps, 1)
                    for p in ((0, 1, 2, 3), (4, 5))[which]:
                        if p == 0:
                            pe.wait_ge(made_pick, 2)
                            pe.wait_ge(z_lo, 6 * l + 6)
                            pe.wait_ge(v_sb, l + 1)
                        if p == 4:
                            pe.wait_ge(ks_act, 3 * l + 1)
                        if p == 5:
                            pe.wait_ge(ks_dve, 3 * l + 1)
                        for a in range(2):
                            h = 2 * p + a
                            last = mm(ps[0:64, K_BANK[p], a * T:(a + 1) * T], pick_k[:, h % G4, :],
                                      zk[:, h // G4, :], start=True, stop=True)
                        last.then_inc(ksel_ps, 1)
                pe.wait_ge(pick_zero, 4)
                pe.wait_ge(made_pick, 6)
                pe.wait_ge(rr_lo_sb, 4 * l + 4)
                for p in range(PAIRS):
                    if p == 0:
                        pe.wait_ge(ks_act, 3 * l + 2)
                    if p == 1:
                        pe.wait_ge(ks_dve, 3 * l + 2)
                    for a in range(2):
                        h = 2 * p + a
                        dst = ps[:, Q_BANK[p], a * T:(a + 1) * T]
                        mm(dst, pick_q[:, h % G4, :], zq[:, h // G4, :], start=True, stop=False)
                        mm(dst, pick_rh[:, h % G4, :], rr_hi[:, h // G4, :], start=False, stop=False)
                        last = mm(dst, pick_rl[:, h % G4, :], rr_lo[:, h // G4, :], start=False, stop=True)
                    last.then_inc(qsel_ps, 1)
                scores(l, 0)
                scores(l, 1)
                scores_t(l, 0)
                for p in range(PAIRS):
                    turn_max(l, p)
                    if p + 2 < PAIRS:
                        scores(l, p + 2)
                    add_max(l, p)
                    if p % 2 == 0 and p >= 2:
                        probs_v(l, p // 2 - 1)
                    if p % 2 == 1 and p >= 3:
                        turn_out(l, (p - 3) // 2)
                    if p + 1 < PAIRS:
                        scores_t(l, p + 1)
                probs_v(l, NG - 1)
                turn_on(l, 0)
                turn_out(l, NG - 1)
                turn_on(l, 1)
                if l == 0:
                    pe.wait_ge(ld_wo, 32)
                for m in range(2):
                    for kc in range(2):
                        pe.wait_ge(ont_sb, 2 * l + kc + 1)
                        k = ON_ROWS[kc]
                        if l == 0:
                            last = mm(ps[0:CH, Y_BANK + m, 0:T], wout[0][0:k, kc, m * CH:(m + 1) * CH],
                                      ont[0:k, kc, :], start=(kc == 0), stop=(kc == 1))
                        else:
                            last = mm(ps[:, Y_BANK + m, 0:C], ont[0:k, kc, m * P:(m + 1) * P],
                                      wout[1][0:k, kc, :], start=(kc == 0), stop=(kc == 1))
                    last.then_inc(y_ps, 1)
                if l == 0:
                    pe.wait_ge(ld_lora, 64)
                    for s in range(2):
                        for k in range(NC):
                            last = pe.transpose(ps[0:RANK, 4, s * C + k * CH:s * C + (k + 1) * CH],
                                                lora_b[:, s, k, :], ident[0:CH, 0:CH])
                    last.then_inc(bt_ps, 1)
                    pe.wait_ge(ld_qkv, 16)
                    for ic in range(NC):
                        for b in range(4):
                            turn(ps[0:CH, 5 + ic, b * CH:(b + 1) * CH], wraw[:, b, ic * CH:(ic + 1) * CH],
                                 b == 0, b == 3)
                    for ic in range(NC):
                        for b in range(2):
                            turn(ps[0:CH, 7, ic * C + b * CH:ic * C + (b + 1) * CH],
                                 wraw[:, 4 + b, ic * CH:(ic + 1) * CH], ic + b == 0, ic + b == 2)


_INS = ["x", "L0_conv_wq", "L0_conv_bq", "L0_conv_wk", "L0_conv_bk", "L0_conv_wv", "L0_conv_bv", "L0_conv_wo",
        "L0_conv_bo", "L0_conv_rel_pos_h", "L0_conv_rel_pos_w", "L1_conv_W_qkv", "L1_conv_b_qkv", "L1_conv_A_q",
        "L1_conv_B_q", "L1_conv_A_v", "L1_conv_B_v", "L1_conv_rel_h", "L1_conv_rel_w", "L1_conv_W_proj",
        "L1_conv_b_proj"]


def kernel(**inputs):
    import numpy as _np
    import concourse.bacc as _bacc
    from concourse import mybir as _mybir
    from concourse.bass_utils import run_bass_kernel_spmd as _run

    nc = _bacc.Bacc("TRN2", target_bir_lowering=False, num_devices=1)
    arrays, args = {}, []
    for name in _INS:
        a = _np.ascontiguousarray(inputs[name])
        arrays[f"in_{name}_dram"] = a
        args.append(nc.dram_tensor(f"in_{name}_dram", a.shape, _mybir.dt.from_np(a.dtype), kind="ExternalInput").ap())
    args.append(nc.dram_tensor("out_0_dram", (1, HW, HW, C), F32, kind="ExternalOutput").ap())
    attention_layers(nc, *args)
    r = _run(nc, [arrays], core_ids=[0])
    return r.results[0]["out_0_dram"]
```

```python
from contextlib import ExitStack

import concourse.bass as bass
from concourse import mybir

F32 = mybir.dt.float32
F32R = mybir.dt.float32r
ALU = mybir.AluOpType
ACT = mybir.ActivationFunctionType
AX = mybir.AxisListType

LAYERS = 2
P = 128
HW = 16
T = HW * HW
TT = T // P
C = 192
CH = 96
NC = C // CH
NH = 12
D = C // NH
G4 = 4
NG = NH // G4
PAIRS = NH // 2
GROUP = C // 32
R = 2 * HW - 1
RANK = 4
EPS = 1e-5
SCALE = [float(D) ** 0.5, float(D) ** -0.5]
LORA_SCALE = 1.0 / RANK
VW = 32


def attention_layers(nc, x, wq, bq, wk, bk, wv, bv, wo, bo, rel_h0, rel_w0,
                     w_qkv, b_qkv, a_q, b_q, a_v, b_v, rel_h1, rel_w1, w_proj, b_proj, out):
    ctx = ExitStack()
    with ctx:
        def sb(name, shape, dt=F32):
            return ctx.enter_context(nc.sbuf_tensor(name, shape, dt))

        def sem(name):
            return ctx.enter_context(nc.semaphore(name))

        ident = sb("ident", [P, P])
        ident_r = sb("ident_r", [P, P], F32R)
        busy = sb("busy", [P, T], mybir.dt.bfloat16)
        anti = sb("anti", [R, R])
        gavg = sb("gavg", [CH, CH])
        gdev = sb("gdev", [CH, CH])
        pow_exp = sb("pow_exp", [CH, NC])
        onehot = sb("onehot", [P, HW, HW])
        head_mask = sb("head_mask", [P, G4])
        pick_q = sb("pick_q", [P, G4, P], F32R)
        pick_k = sb("pick_k", [P, G4, 64], F32R)
        pick_rh = sb("pick_rh", [P, G4, P], F32R)
        pick_rl = sb("pick_rl", [P, G4, P], F32R)
        ones4_raw = sb("ones4_raw", [4, 2, P])
        ones4 = sb("ones4", [4, 2, P], F32R)
        wqk = [sb(f"wqk{l}", [CH + 1, NC, 2 * C]) for l in range(LAYERS)]
        wvv = [sb(f"wvv{l}", [CH + 1, NC, C]) for l in range(LAYERS)]
        wout = [sb(f"wout{l}", [P, 2, C]) for l in range(LAYERS)]
        wraw = sb("wraw", [CH, 6, C])
        wpraw = sb("wpraw", [CH, NC, C])
        lora_a = sb("lora_a", [RANK, 2, C])
        lora_b = sb("lora_b", [CH, 2, NC, RANK])
        lora_bt = sb("lora_bt", [RANK, 2, C])
        rel_raw = sb("rel_raw", [R, 4, D])
        rel_rep = sb("rel_rep", [R, 4, 8, D])
        rel_hi = sb("rel_hi", [P, LAYERS, 2 * R], F32R)
        rel_lo = sb("rel_lo", [P, LAYERS, 2 * R], F32R)
        table = [sb(f"table{l}", [P, 2, 2, R, G4], F32R) for l in range(LAYERS)]
        xin = sb("xin", [P, TT, C])
        xt = [sb(f"xt{l}", [CH, NC, T]) for l in range(LAYERS)]
        stats = sb("stats", [CH, LAYERS, NC, 6])
        mv = sb("mv", [CH, LAYERS, NC, 2])
        warm = sb("warm", [1, 1])
        gmean = sb("gmean", [CH, LAYERS, NC])
        ev = sb("ev", [CH, LAYERS, NC])
        vare = sb("vare", [CH, LAYERS, NC])
        rstd = sb("rstd", [CH, LAYERS, NC])
        xn = sb("xn", [CH + 1, NC, T])
        zq = sb("zq", [P, NG, T], F32R)
        zk = sb("zk", [P, NG, T], F32R)
        va = sb("va", [P, TT, NH, VW])
        rr_hi = sb("rr_hi", [P, NG, T], F32R)
        rr_lo = sb("rr_lo", [P, NG, T], F32R)
        qs = sb("qs", [P, NH, T], F32R)
        ks = sb("ks", [P, NH, T], F32R)
        nm = sb("nm", [P, PAIRS, 2, TT])
        nmhl = sb("nmhl", [P, PAIRS, TT, 2, 2], F32R)
        nmt = sb("nmt", [4, PAIRS, T], F32R)
        pt = sb("pt", [P, PAIRS, 2, TT, T])
        ot = sb("ot", [P, NG, T])
        rinv = sb("rinv", [P, NG, TT, G4])
        on = sb("on", [P, TT, C])
        ont = sb("ont", [P, 2, T])
        res = sb("res", [P, TT, C])

        ps = ctx.enter_context(nc.psum_tensor("ps", [P, 8, 512], F32))

        ld_x, ld_wqk, ld_wv, ld_rel, ld_wo, ld_qkv = (sem(n) for n in (
            "ld_x", "ld_wqk", "ld_wv", "ld_rel", "ld_wo", "ld_qkv"))
        ld_b1, ld_lora, ld_proj, ld_bproj, stored = (sem(n) for n in (
            "ld_b1", "ld_lora", "ld_proj", "ld_bproj", "stored"))
        zeroed, made_ident, made_anti, made_gavg, made_ones4, made_xones, made_va = (sem(n) for n in (
            "zeroed", "made_ident", "made_anti", "made_gavg", "made_ones4", "made_xones", "made_va"))
        made_gdev, made_mask, made_pick, made_rep = (sem(n) for n in (
            "made_gdev", "made_mask", "made_pick", "made_rep"))
        pick_zero, made_keys, made_ident_r, made_busy = (sem(n) for n in (
            "pick_zero", "made_keys", "made_ident_r", "made_busy"))
        (xt_ps, tab_ps, gn_ps, qk_ps, v_ps, rel_ps, ksel_ps, qsel_ps, s_ps, st_ps, nmt_ps, o_ps,
         oq_ps, ont_ps, y_ps, bt_ps, wt_ps, wpt_ps) = (sem(n) for n in (
            "xt_ps", "tab_ps", "gn_ps", "qk_ps", "v_ps", "rel_ps", "ksel_ps", "qsel_ps", "s_ps",
            "st_ps", "nmt_ps", "o_ps", "oq_ps", "ont_ps", "y_ps", "bt_ps", "wt_ps", "wpt_ps"))
        (warmed, xt_sb, relhi_sb, z_hi, rr_hi_sb, ks_act, qs_act, nmt_sb, p_sb, ont_sb,
         wv_sb, wpt_sb, res_act) = (sem(n) for n in (
            "warmed", "xt_sb", "relhi_sb", "z_hi", "rr_hi_sb", "ks_act", "qs_act", "nmt_sb", "p_sb",
            "ont_sb", "wv_sb", "wpt_sb", "res_act"))
        (rello_sb, tab_sb, bn, var_sb, ev_sb, mean_sb, xn_sb, z_lo, v_sb, rr_lo_sb, ks_dve, qs_dve,
         max_sb, nm_hi, nm_lo, ot_sb, ri_sb, on_sb, bt_sb, wt_sb, res_dve) = (sem(n) for n in (
            "rello_sb", "tab_sb", "bn", "var_sb", "ev_sb", "mean_sb", "xn_sb", "z_lo", "v_sb",
            "rr_lo_sb", "ks_dve", "qs_dve", "max_sb", "nm_hi", "nm_lo", "ot_sb", "ri_sb", "on_sb",
            "bt_sb", "wt_sb", "res_dve"))
        rstd_sb = sem("rstd_sb")

        X_BANK = [[0, 1], [2, 3]]
        GN_BANK, VAR_BANK = [4, 5], [5, 0]
        V_BANK = 3
        REL_BANK = 4
        K_BANK = [0, 1, 2, 3, 0, 1]
        Q_BANK = [2, 3, 7, 4, 5, 6]
        S_BANK = [0, 1]
        ST_BANK = [2, 4]
        O_BANK, NM_BANK = [6, 6, 1], 7
        ONT_BANK = [7, 4]
        Y_BANK = 2
        BT_BANK, WQK_BANK, WV_BANK, WP_BANK = 0, 0, 6, 7
        BUSY_BEFORE_QK = [4, 34]
        BUSY_BANK = [7, 4]
        K_ACT, K_DVE = (0, 2, 4), (1, 3, 5)
        Q_ACT, Q_DVE = (0, 2, 3, 4, 5), (1,)
        ON_ROWS = [P, C - P]

        tokens = x.rearrange("b h w c -> (b h w) c").rearrange("(t p) c -> p t c", p=P)
        out_tokens = out.rearrange("b h w c -> (b h w) c").rearrange("(t p) c -> p t c", p=P)

        def row(v):
            return v.rearrange("(a n) -> a n", a=1)

        def chunks(w):
            return w.rearrange("(k p) n -> p k n", p=CH)

        block = ctx.enter_context(nc.Block())

        @block.sync
        def _(sp):
            sp.dma_start(xin[:, :, :], tokens).then_inc(ld_x, 16)
            for n, rel in enumerate((rel_h0, rel_w0, rel_h1, rel_w1)):
                sp.dma_start(rel_raw[:, n, :], rel).then_inc(ld_rel, 16)
            sp.dma_start(wqk[0][0:CH, :, 0:C], chunks(wq)).then_inc(ld_wqk, 16)
            sp.dma_start(wqk[0][0:CH, :, C:2 * C], chunks(wk)).then_inc(ld_wqk, 16)
            sp.dma_start(wqk[0][CH:CH + 1, 0, 0:C], row(bq)).then_inc(ld_wqk, 16)
            sp.dma_start(wqk[0][CH:CH + 1, 0, C:2 * C], row(bk)).then_inc(ld_wqk, 16)
            sp.dma_start(wvv[0][0:CH, :, :], chunks(wv)).then_inc(ld_wv, 16)
            sp.dma_start(wvv[0][CH:CH + 1, 0, :], row(bv)).then_inc(ld_wv, 16)
            sp.dma_start(wraw[:, :, :], chunks(w_qkv)).then_inc(ld_qkv, 16)
            for s, (a, b) in enumerate(((a_q, b_q), (a_v, b_v))):
                sp.dma_start(lora_a[:, s, :], a).then_inc(ld_lora, 16)
                sp.dma_start(lora_b[:, s, :, :], chunks(b)).then_inc(ld_lora, 16)
            sp.dma_start(wout[0][:, 0, :], wo[0:P, :]).then_inc(ld_wo, 16)
            sp.dma_start(wout[0][0:C - P, 1, :], wo[P:C, :]).then_inc(ld_wo, 16)
            sp.dma_start(wout[0][C - P:C - P + 1, 1, :], row(bo)).then_inc(ld_wo, 16)
            sp.dma_start(wpraw[:, :, :], chunks(w_proj)).then_inc(ld_proj, 16)
            sp.dma_start(wqk[1][CH:CH + 1, 0, :], row(b_qkv)[:, 0:2 * C]).then_inc(ld_b1, 16)
            sp.dma_start(wvv[1][CH:CH + 1, 0, :], row(b_qkv)[:, 2 * C:3 * C]).then_inc(ld_b1, 16)
            sp.dma_start(wout[1][C - P:C - P + 1, 1, :], row(b_proj)).then_inc(ld_bproj, 16)
            sp.wait_ge(res_act, 1)
            sp.wait_ge(res_dve, 1)
            sp.dma_start(out_tokens, res[:, :, :]).then_inc(stored, 16)
            sp.wait_ge(stored, 16)

        def rel_src(which, half):
            v = ps[0:64, REL_BANK + 2 * which + half, 0:8 * NG * HW]
            if which == 0:
                return v.rearrange("p (h g w) -> p g h w", g=NG, w=HW)
            return v.rearrange("p (w g h) -> p g h w", g=NG, h=HW)

        def rel_dst(tile, which, half):
            v = tile[64 * which:64 * which + 64, :, :].rearrange("p g (h w) -> p g h w", w=HW)
            return v[:, :, 8 * half:8 * half + 8, :] if which == 0 else v[:, :, :, 8 * half:8 * half + 8]

        def chunk_rows(which, g):
            m = 64 * (g + NG * which)
            return ps[m % P:m % P + 64, m // P, 0:T]

        @block.gpsimd
        def _(pool):
            def inverse_deviation(l):
                pool.wait_ge(var_sb, l + 1)
                pool.tensor_tensor(rstd[:, l, :], vare[:, l, :], pow_exp[:, :],
                                   ALU.pow).then_inc(rstd_sb, 1)

            pool.memset(ident[:, :], 0.0).then_inc(zeroed, 1)
            pool.wait_ge(zeroed, 1)
            pool.affine_select(out=ident[:, :], in_=ident[:, :], compare_op=ALU.not_equal, fill=1.0,
                               base=0, pattern=[[-1, P]], channel_multiplier=1).then_inc(made_ident, 1)
            pool.memset(gavg[:, :], 1.0 / GROUP).then_inc(zeroed, 1)
            pool.memset(anti[:, :], 0.0).then_inc(zeroed, 1)
            pool.wait_ge(zeroed, 3)
            pool.affine_select(out=anti[:, :], in_=anti[:, :], compare_op=ALU.not_equal, fill=1.0,
                               base=-(R - 1), pattern=[[1, R]], channel_multiplier=1).then_inc(made_anti, 1)
            gv = gavg[:, :].rearrange("p (g k) -> p g k", k=GROUP)
            pool.affine_select(out=gv, in_=gv, compare_op=ALU.is_ge, fill=0.0, base=0,
                               pattern=[[-GROUP, CH // GROUP], [0, GROUP]],
                               channel_multiplier=1).then_inc(zeroed, 1)
            pool.wait_ge(zeroed, 4)
            pool.affine_select(out=gv, in_=gv, compare_op=ALU.is_ge, fill=0.0, base=GROUP - 1,
                               pattern=[[GROUP, CH // GROUP], [0, GROUP]],
                               channel_multiplier=-1).then_inc(made_gavg, 1)
            pool.memset(pow_exp[:, :], -0.5).then_inc(zeroed, 1)
            pool.memset(onehot[:, :, :], 0.0).then_inc(zeroed, 1)
            for n, steps in enumerate(([-1, 0], [0, -1], [-1, 0], [0, -1])):
                pool.wait_ge(zeroed, 6 + n)
                pool.affine_select(out=onehot[:, :, :], in_=onehot[:, :, :], compare_op=ALU.not_equal,
                                   fill=1.0, base=-(64 + D * n), pattern=[[s_, HW] for s_ in steps],
                                   channel_multiplier=1).then_inc(zeroed, 1)
            inverse_deviation(0)
            pool.memset(va[:, :, :, D:VW], 0.0).then_inc(zeroed, 1)
            pool.memset(ones4_raw[:, :, :], 1.0).then_inc(zeroed, 1)
            pool.wait_ge(zeroed, 12)
            pool.memset(va[:, :, :, D:D + 1], 1.0).then_inc(made_va, 1)
            pool.affine_select(out=ones4_raw[:, :, :], in_=ones4_raw[:, :, :],
                               compare_op=ALU.is_ge, fill=0.0, base=0, pattern=[[-2, 2], [0, P]],
                               channel_multiplier=1).then_inc(zeroed, 1)
            pool.wait_ge(zeroed, 13)
            pool.affine_select(out=ones4[:, :, :], in_=ones4_raw[:, :, :],
                               compare_op=ALU.is_ge, fill=0.0, base=1, pattern=[[2, 2], [0, P]],
                               channel_multiplier=-1).then_inc(made_ones4, 1)
            inverse_deviation(1)

        @block.scalar
        def _(act):
            def copy(dst, src, scale=1.0):
                return act.activation(dst, src, ACT.Copy, scale=scale)

            def layer_input(l):
                for ic in range(NC):
                    act.wait_ge(bn, 4 * l + ic + 1)
                    copy(xt[l][:, ic, :], ps[0:CH, X_BANK[l][ic], 0:T]).then_inc(xt_sb, 1)

            act.activation(warm[:, :], nc.const_aps.scalar_like(0.0, warm[:, :]), ACT.Exp).then_inc(warmed, 1)
            layer_input(0)
            act.wait_ge(ld_rel, 64)
            for n in range(4):
                copy(rel_rep[:, n, :, :],
                     rel_raw[:, n, :].unsqueeze(1).to_broadcast([R, 8, D])).then_inc(made_rep, 1)
            act.wait_ge(made_ident, 1)
            by_head = ident[:, :].rearrange("p (s j c) -> p j s c", s=2, j=G4)
            by_pos = ident[:, :].rearrange("p (k j) -> p j k", j=G4)
            copy(ident_r[:, :], ident[:, :]).then_inc(made_ident_r, 1)
            for n in range(2):
                copy(pick_k[:, :, :].rearrange("p j (s r c) -> p r j s c", s=2, r=2)[:, n],
                     by_head).then_inc(made_pick, 1)
            act.wait_ge(tab_ps, 1)
            for l in range(LAYERS):
                copy(rel_hi[:, l, :], ps[:, 3, l * 2 * R:(l + 1) * 2 * R],
                     scale=1.0 / SCALE[l]).then_inc(relhi_sb, 1)
            for n in range(2):
                copy(pick_q[:, :, 0:64].rearrange("p j (r s c) -> p r j s c", s=2, r=2)[:, n],
                     by_head).then_inc(made_pick, 1)
            copy(pick_rh[:, :, 64:96], by_pos).then_inc(made_pick, 1)
            copy(pick_rl[:, :, 96:128], by_pos).then_inc(made_pick, 1)

            def key_onehots(n):
                act.wait_ge(zeroed, 10)
                copy(ks[64:P, 3 * n:3 * n + 3, :], onehot[64:P, :, :].rearrange("p a b -> p (a b)")
                     .unsqueeze(1).to_broadcast([64, 3, T])).then_inc(made_keys, 1)

            def key_tiles(l, p):
                act.wait_ge(ksel_ps, PAIRS * l + p + 1)
                copy(ks[0:64, 2 * p:2 * p + 2, :].rearrange("p a t -> p (a t)"),
                     ps[0:64, K_BANK[p], :]).then_inc(ks_act, 1)

            def query_tiles(l, p):
                act.wait_ge(qsel_ps, PAIRS * l + p + 1)
                copy(qs[:, 2 * p:2 * p + 2, :].rearrange("p a t -> p (a t)"),
                     ps[:, Q_BANK[p], :]).then_inc(qs_act, 1)

            def max_rows(l, p):
                act.wait_ge(nmt_ps, PAIRS * l + p + 1)
                copy(nmt[:, p, :], ps[0:4, NM_BANK, 0:T]).then_inc(nmt_sb, 1)

            def probabilities(l, p):
                act.wait_ge(st_ps, PAIRS * l + p + 1)
                act.activation(pt[:, p, :, :, :].rearrange("p a k t -> p a (k t)"),
                               ps[:, ST_BANK[p % 2]:ST_BANK[p % 2] + 2, :], ACT.Exp,
                               scale=SCALE[l]).then_inc(p_sb, 1)

            for l in range(LAYERS):
                if l == 1:
                    layer_input(1)
                    act.wait_ge(wt_ps, 3)
                    copy(wvv[1][0:CH, :, :].rearrange("p k n -> p (k n)"),
                         ps[0:CH, WV_BANK, 0:2 * C]).then_inc(wv_sb, 1)
                    act.wait_ge(wpt_ps, 1)
                    copy(wout[1][:, 0, :], ps[:, WP_BANK, 0:C]).then_inc(wpt_sb, 1)
                    copy(wout[1][0:C - P, 1, :], ps[0:C - P, WP_BANK, C:2 * C]).then_inc(wpt_sb, 1)
                for which in range(2):
                    for g in range(NG):
                        act.wait_ge(qk_ps, 3 * l + (64 * (g + NG * which)) // P + 1)
                        copy((zq, zk)[which][0:64, g, :], chunk_rows(which, g)).then_inc(z_hi, 1)
                    if l == 0:
                        key_onehots(2 * which)
                        key_onehots(2 * which + 1)
                for which in range(2):
                    for half in range(2):
                        act.wait_ge(rel_ps, 4 * l + 2 * which + half + 1)
                        copy(rel_dst(rr_hi, which, half), rel_src(which, half)).then_inc(rr_hi_sb, 1)
                    if which == 0:
                        key_tiles(l, 0)
                        key_tiles(l, 2)
                    else:
                        key_tiles(l, 4)
                for p in (0, 2, 3, 4):
                    query_tiles(l, p)
                max_rows(l, 0)
                query_tiles(l, 5)
                for p in range(PAIRS):
                    if p == 0:
                        max_rows(l, 1)
                    probabilities(l, p)
                    if p + 2 < PAIRS:
                        max_rows(l, p + 2)
                for kc in range(2):
                    act.wait_ge(ont_ps, 2 * l + kc + 1)
                    copy(ont[0:ON_ROWS[kc], kc, :],
                         ps[0:ON_ROWS[kc], ONT_BANK[kc], 0:T]).then_inc(ont_sb, 1)
            act.wait_ge(y_ps, NC + 1)
            copy(res[:, 0, :], ps[:, Y_BANK, 0:C]).then_inc(res_act, 1)

        @block.vector
        def _(dve):
            dve.memset(busy[:, :], 0.0).then_inc(made_busy, 1)
            dve.memset(xn[CH:CH + 1, 0, :], 1.0).then_inc(made_xones, 1)
            dve.memset(ont[C - P:C - P + 1, 1, :], 1.0).then_inc(made_xones, 1)
            dve.memset(pick_q[:, :, 64:P].bitcast(F32), 0.0).then_inc(pick_zero, 1)
            dve.memset(pick_rh[:, :, 0:64].bitcast(F32), 0.0).then_inc(pick_zero, 1)
            dve.memset(pick_rh[:, :, 96:P].bitcast(F32), 0.0).then_inc(pick_zero, 1)
            dve.memset(pick_rl[:, :, 0:96].bitcast(F32), 0.0).then_inc(pick_zero, 1)
            dve.wait_ge(made_ident, 1)
            dve.tensor_reduce(head_mask[:, :], ident[:, :].rearrange("p (s j c) -> p j s c", s=2, j=G4),
                              AX.XY, ALU.add).then_inc(made_mask, 1)
            dve.wait_ge(made_gavg, 1)
            dve.tensor_tensor(gdev[:, :], ident[0:CH, 0:CH], gavg[:, :], ALU.subtract).then_inc(made_gdev, 1)

            def key_tiles(l, p):
                dve.wait_ge(ksel_ps, PAIRS * l + p + 1)
                dve.tensor_copy(ks[0:64, 2 * p:2 * p + 2, :].rearrange("p a t -> p (a t)"),
                                ps[0:64, K_BANK[p], :]).then_inc(ks_dve, 1)

            def normalise(l, g):
                dve.wait_ge(oq_ps, NG * l + g + 1)
                q = ps[:, O_BANK[g], T:2 * T].rearrange("p (t j d) -> p t j d", t=TT, j=G4)
                dve.reciprocal(rinv[:, g, :, :], q[:, :, :, D]).then_inc(ri_sb, 1)
                dve.wait_ge(ri_sb, NG * l + g + 1)
                dve.tensor_tensor(
                    on[:, :, 64 * g:64 * g + 64].rearrange("p t (j d) -> p t j d", d=D), q[:, :, :, 0:D],
                    rinv[:, g, :, :].unsqueeze(3).to_broadcast([P, TT, G4, D]), ALU.mult).then_inc(on_sb, 1)

            def query_tiles(l, p):
                dve.wait_ge(qsel_ps, PAIRS * l + p + 1)
                dve.tensor_copy(qs[:, 2 * p:2 * p + 2, :].rearrange("p a t -> p (a t)"),
                                ps[:, Q_BANK[p], :]).then_inc(qs_dve, 1)

            def maxima(l, p):
                for a in range(2):
                    dve.wait_ge(s_ps, NH * l + 2 * p + a + 1)
                    dve.tensor_reduce(nm[:, p, a, :], ps[:, S_BANK[a], :].rearrange("p (t k) -> p t k", k=T),
                                      AX.X, ALU.max, negate=True).then_inc(max_sb, 1)
                by_tile = nm[:, p, :, :].rearrange("p a t -> p t a")
                dve.wait_ge(max_sb, NH * l + 2 * p + 2)
                dve.tensor_copy(nmhl[:, p, :, :, 0], by_tile).then_inc(nm_hi, 1)
                dve.wait_ge(nm_hi, PAIRS * l + p + 1)
                dve.tensor_tensor(nmhl[:, p, :, :, 1], by_tile, nmhl[:, p, :, :, 0].bitcast(F32),
                                  ALU.subtract).then_inc(nm_lo, 1)

            def out_columns(l, n):
                g, r0, r1 = ((0, 0, P), (1, 0, P), (2, 0, 64), (2, 64, P))[n]
                dve.wait_ge(o_ps, 4 * l + n + 1)
                dve.tensor_copy(ot[r0:r1, g, :], ps[r0:r1, O_BANK[g], 0:T]).then_inc(ot_sb, 1)

            for l in range(LAYERS):
                for ic in range(NC):
                    dve.wait_ge((xt_ps, y_ps)[l], ic + 1)
                    dve.bn_stats(stats[:, l, ic, :], ps[0:CH, X_BANK[l][ic], 0:T]).then_inc(bn, 1)
                for ic in range(NC):
                    dve.wait_ge(bn, 4 * l + ic + 1)
                    dve.bn_aggr(mv[:, l, ic, :], stats[:, l, ic, :]).then_inc(bn, 1)
                dve.wait_ge(bn, 4 * l + 4)
                dve.wait_ge(gn_ps, 2 * l + 1)
                for ic in range(NC):
                    dev = ps[0:CH, GN_BANK[l], 2 + ic:3 + ic]
                    dve.scalar_tensor_tensor(out=ev[:, l, ic:ic + 1], in0=dev, scalar=dev,
                                             in1=mv[:, l, ic, 1:2],
                                             op0=ALU.mult, op1=ALU.add).then_inc(ev_sb, 1)
                dve.tensor_copy(gmean[:, l, :], ps[0:CH, GN_BANK[l], 0:2]).then_inc(mean_sb, 1)
                dve.wait_ge(gn_ps, 2 * l + 2)
                dve.tensor_scalar(vare[:, l, :], ps[0:CH, VAR_BANK[l], 0:2], EPS, None,
                                  ALU.add).then_inc(var_sb, 1)
                dve.wait_ge(mean_sb, l + 1)
                dve.wait_ge(xt_sb, NC * l + NC)
                dve.wait_ge(rstd_sb, l + 1)
                for ic in range(NC):
                    dve.tensor_scalar(xn[0:CH, ic, :], xt[l][:, ic, :], gmean[:, l, ic:ic + 1],
                                      rstd[:, l, ic:ic + 1], ALU.subtract, ALU.mult).then_inc(xn_sb, 1)
                if l == 0:
                    dve.wait_ge(relhi_sb, LAYERS)
                    for k in range(LAYERS):
                        dve.scalar_tensor_tensor(out=rel_lo[:, k, :], in0=ps[:, 3, k * 2 * R:(k + 1) * 2 * R],
                                                 scalar=1.0 / SCALE[k], in1=rel_hi[:, k, :].bitcast(F32),
                                                 op0=ALU.mult, op1=ALU.subtract).then_inc(rello_sb, 1)
                    dve.wait_ge(made_mask, 1)
                    for k in range(LAYERS):
                        dve.wait_ge(rello_sb, k + 1)
                        for part, half in enumerate((rel_hi, rel_lo)):
                            dve.tensor_tensor(
                                table[k][:, part, :, :, :].rearrange("p s r j -> p (s r) j"),
                                half[:, k, :].bitcast(F32).unsqueeze(2).to_broadcast([P, 2 * R, G4]),
                                head_mask[:, :].unsqueeze(1).to_broadcast([P, 2 * R, G4]),
                                ALU.mult).then_inc(tab_sb, 1)
                for which in range(2):
                    for g in range(NG):
                        z = (zq, zk)[which]
                        dve.wait_ge(z_hi, 6 * l + NG * which + g + 1)
                        dve.tensor_tensor(z[64:P, g, :], chunk_rows(which, g), z[0:64, g, :].bitcast(F32),
                                          ALU.subtract).then_inc(z_lo, 1)
                dve.wait_ge(v_ps, l + 1)
                dve.tensor_copy(va[:, :, :, 0:D], ps[:, V_BANK, 0:TT * C].rearrange(
                    "p (t h d) -> p t h d", t=TT, d=D)).then_inc(v_sb, 1)
                for which in range(2):
                    for half in range(2):
                        n = 4 * l + 2 * which + half + 1
                        dve.wait_ge(rr_hi_sb, n)
                        dve.tensor_tensor(rel_dst(rr_lo, which, half), rel_src(which, half),
                                          rel_dst(rr_hi, which, half).bitcast(F32),
                                          ALU.subtract).then_inc(rr_lo_sb, 1)
                    if which == 0:
                        key_tiles(l, 1)
                    else:
                        key_tiles(l, 3)
                        key_tiles(l, 5)
                query_tiles(l, 1)
                for p in range(PAIRS):
                    maxima(l, p)
                out_columns(l, 0)
                if l == 0:
                    dve.wait_ge(bt_ps, 1)
                    dve.tensor_scalar(lora_bt[:, :, :].rearrange("p a n -> p (a n)"),
                                      ps[0:RANK, BT_BANK, 0:2 * C], LORA_SCALE, None,
                                      ALU.mult).then_inc(bt_sb, 1)
                normalise(l, 0)
                out_columns(l, 1)
                if l == 0:
                    dve.wait_ge(wt_ps, 1)
                    dve.tensor_copy(wqk[1][0:CH, 0, :], ps[0:CH, WQK_BANK, 0:2 * C]).then_inc(wt_sb, 1)
                normalise(l, 1)
                out_columns(l, 2)
                if l == 0:
                    dve.wait_ge(wt_ps, 2)
                    dve.tensor_copy(wqk[1][0:CH, 1, :], ps[0:CH, WQK_BANK, 0:2 * C]).then_inc(wt_sb, 1)
                out_columns(l, 3)
                normalise(l, 2)
            dve.wait_ge(y_ps, NC + 2)
            dve.tensor_copy(res[:, 1, :], ps[:, Y_BANK + 1, 0:C]).then_inc(res_dve, 1)

        @block.tensor
        def _(pe):
            mm = pe.matmul

            def keep_busy(l, n):
                for _ in range(n):
                    mm(ps[:, BUSY_BANK[l], 0:P], busy[:, 0:P], busy[:, 0:P], start=True, stop=True)

            pe.wait_ge(made_busy, 1)
            keep_busy(0, 20)
            pe.wait_ge(ld_x, 16)
            pe.wait_ge(made_ident, 1)
            for ic in range(NC):
                for t in range(TT):
                    last = pe.transpose(ps[0:CH, ic, t * P:(t + 1) * P], xin[:, t, ic * CH:(ic + 1) * CH],
                                        ident[:, :])
                last.then_inc(xt_ps, 1)
            keep_busy(0, 7)

            def relative_tables():
                pe.wait_ge(made_anti, 1)
                pe.wait_ge(made_rep, 4)
                for n in range(4):
                    last = mm(ps[:, 3, n * R:(n + 1) * R], rel_rep[:, n, :, :].rearrange("r b c -> r (b c)"),
                              anti[:, :], start=True, stop=True)
                last.then_inc(tab_ps, 1)

            def group_means(l):
                pe.wait_ge(bn, 4 * l + 4)
                pe.wait_ge(made_gavg, 1)
                pe.wait_ge(made_gdev, 1)
                mm(ps[0:CH, GN_BANK[l], 0:2], gavg[:, :], mv[:, l, :, 0], start=True, stop=True)
                mm(ps[0:CH, GN_BANK[l], 2:4], gdev[:, :], mv[:, l, :, 0], start=True,
                   stop=True).then_inc(gn_ps, 1)

            def group_variance(l):
                pe.wait_ge(ev_sb, 2 * l + 2)
                mm(ps[0:CH, VAR_BANK[l], 0:2], gavg[:, :], ev[:, l, :], start=True,
                   stop=True).then_inc(gn_ps, 1)

            def turn(dst, src, first, last):
                return mm(dst, src, ident[0:CH, 0:CH], start=first, stop=last, is_transpose=True,
                          skip_group_check=True)

            def keys_out(l, p):
                if p in K_ACT:
                    pe.wait_ge(ks_act, len(K_ACT) * l + K_ACT.index(p) + 1)
                else:
                    pe.wait_ge(ks_dve, len(K_DVE) * l + K_DVE.index(p) + 1)

            def queries_out(l, p):
                if p in Q_ACT:
                    pe.wait_ge(qs_act, len(Q_ACT) * l + Q_ACT.index(p) + 1)
                else:
                    pe.wait_ge(qs_dve, len(Q_DVE) * l + Q_DVE.index(p) + 1)

            def query_rows(l, p):
                if Q_BANK[p] < 4:
                    keys_out(l, K_BANK.index(Q_BANK[p]))
                else:
                    pe.wait_ge(rr_lo_sb, 4 * l + 4)
                for a in range(2):
                    h = 2 * p + a
                    mm(ps[:, Q_BANK[p], a * T:(a + 1) * T], pick_q[:, h % G4, :], zq[:, h // G4, :],
                       start=(a == 0), stop=False, skip_group_check=True)

            def relative_rows(l, p):
                for part, (pick, rr, split) in enumerate(((pick_rh, rr_hi, rr_hi_sb), (pick_rl, rr_lo, rr_lo_sb))):
                    pe.wait_ge(split, 4 * l + 4)
                    for a in range(2):
                        h = 2 * p + a
                        last = mm(ps[:, Q_BANK[p], a * T:(a + 1) * T], pick[:, h % G4, :], rr[:, h // G4, :],
                                  start=False, stop=(part == 1), skip_group_check=True)
                last.then_inc(qsel_ps, 1)

            def query_select(l, p):
                query_rows(l, p)
                relative_rows(l, p)

            def scores(l, p):
                if p == 0:
                    pe.wait_ge(made_keys, 4)
                    for k in range(PAIRS):
                        keys_out(l, k)
                queries_out(l, p)
                for a in range(2):
                    if p >= 1:
                        pe.wait_ge(max_sb, NH * l + 2 * p + a - 1)
                    for t in range(TT):
                        last = mm(ps[:, S_BANK[a], t * T:(t + 1) * T],
                                  qs[:, 2 * p + a, t * P:(t + 1) * P], ks[:, 2 * p + a, :],
                                  start=True, stop=True)
                    last.then_inc(s_ps, 1)

            def scores_t(l, p):
                if p < 2:
                    for q in range(PAIRS):
                        if ST_BANK[p] <= Q_BANK[q] < ST_BANK[p] + 2:
                            queries_out(l, q)
                else:
                    pe.wait_ge(p_sb, PAIRS * l + p - 1)
                for a in range(2):
                    for t in range(TT):
                        mm(ps[:, ST_BANK[p % 2] + a, t * T:(t + 1) * T],
                           ks[:, 2 * p + a, t * P:(t + 1) * P], qs[:, 2 * p + a, :],
                           start=(t == 0), stop=False, skip_group_check=True)

            def turn_max(l, p):
                if p == 0:
                    pe.wait_ge(made_ident_r, 1)
                    queries_out(l, Q_BANK.index(NM_BANK))
                else:
                    pe.wait_ge(nmt_sb, PAIRS * l + p)
                pe.wait_ge(nm_lo, PAIRS * l + p + 1)
                for t in range(TT):
                    last = mm(ps[0:4, NM_BANK, t * P:(t + 1) * P],
                              nmhl[:, p, t, :, :].rearrange("p a s -> p (a s)"), ident_r[:, :],
                              start=True, stop=True)
                last.then_inc(nmt_ps, 1)

            def add_max(l, p):
                if l == 0 and p == 0:
                    pe.wait_ge(made_ones4, 1)
                pe.wait_ge(nmt_sb, PAIRS * l + p + 1)
                for a in range(2):
                    for t in range(TT):
                        last = mm(ps[:, ST_BANK[p % 2] + a, t * T:(t + 1) * T], ones4[:, a, :], nmt[:, p, :],
                                  start=False, stop=True, skip_group_check=True)
                last.then_inc(st_ps, 1)

            def probs_v(l, n):
                g, heads = ((0, (0, 1, 2, 3)), (1, (0, 1, 2, 3)), (2, (0, 1)), (2, (2, 3)))[n]
                if n == 0:
                    queries_out(l, Q_BANK.index(O_BANK[0]))
                    pe.wait_ge(v_sb, l + 1)
                    pe.wait_ge(made_va, 1)
                elif n == 1:
                    pe.wait_ge(on_sb, NG * l + 1)
                elif n == 2:
                    pe.wait_ge(max_sb, NH * l + NH)
                pe.wait_ge(p_sb, PAIRS * l + (2, 4, 5, 6)[n])
                for t in range(TT):
                    for j in heads:
                        last = mm(ps[32 * j:32 * j + 32, O_BANK[g], 0:T], va[:, t, G4 * g + j, :],
                                  pt[:, 2 * g + j // 2, j % 2, t, :], start=(t == 0), stop=(t == TT - 1))
                last.then_inc(o_ps, 1)

            def turn_out(l, g):
                pe.wait_ge(ot_sb, 4 * l + (1, 2, 4)[g])
                for t in range(TT):
                    last = pe.transpose(ps[:, O_BANK[g], T + t * P:T + (t + 1) * P],
                                        ot[:, g, t * P:(t + 1) * P], ident[:, :])
                last.then_inc(oq_ps, 1)

            def turn_on(l, kc):
                pe.wait_ge(on_sb, NG * l + 2 + kc)
                for t in range(TT):
                    last = pe.transpose(ps[0:ON_ROWS[kc], ONT_BANK[kc], t * P:(t + 1) * P],
                                        on[:, t, kc * P:kc * P + ON_ROWS[kc]], ident[:, :])
                last.then_inc(ont_ps, 1)

            def residual(l):
                pe.wait_ge(p_sb, PAIRS * l + PAIRS - 1)
                pe.wait_ge(xt_sb, NC * l + NC)
                for m in range(2):
                    for n in range(2):
                        if l == 0:
                            mm(ps[0:CH, Y_BANK + m, n * P:(n + 1) * P], xin[:, n, m * CH:(m + 1) * CH],
                               ident[:, :], start=(n == 0), stop=False, is_transpose=True,
                               skip_group_check=True)
                        else:
                            mm(ps[:, Y_BANK + m, n * CH:(n + 1) * CH], xt[1][:, n, m * P:(m + 1) * P],
                               ident[0:CH, 0:CH], start=(n == 0), stop=False, is_transpose=True,
                               skip_group_check=True)

            def output_product(l, kc, m):
                k = ON_ROWS[kc] + kc
                if l == 0:
                    return mm(ps[0:CH, Y_BANK + m, 0:T], wout[0][0:k, kc, m * CH:(m + 1) * CH],
                              ont[0:k, kc, :], start=False, stop=(kc == 1), skip_group_check=True)
                return mm(ps[:, Y_BANK + m, 0:C], ont[0:k, kc, m * P:(m + 1) * P],
                          wout[1][0:k, kc, :], start=False, stop=(kc == 1), skip_group_check=True)

            def lora_columns():
                pe.wait_ge(ld_lora, 64)
                pe.wait_ge(max_sb, NH)
                for s in range(2):
                    for k in range(NC):
                        last = pe.transpose(ps[0:RANK, BT_BANK, s * C + k * CH:s * C + (k + 1) * CH],
                                            lora_b[:, s, k, :], ident[0:CH, 0:CH])
                last.then_inc(bt_ps, 1)

            def qk_weights(ic):
                pe.wait_ge(ld_qkv, 16)
                pe.wait_ge(bt_sb, 1)
                if ic == 1:
                    pe.wait_ge(wt_sb, 1)
                for b in range(4):
                    turn(ps[0:CH, WQK_BANK, b * CH:(b + 1) * CH], wraw[:, b, ic * CH:(ic + 1) * CH],
                         b == 0, b == 3)
                mm(ps[0:CH, WQK_BANK, 0:C], lora_a[:, 0, ic * CH:(ic + 1) * CH], lora_bt[:, 0, :],
                   start=False, stop=True, skip_group_check=True).then_inc(wt_ps, 1)

            def v_weights():
                pe.wait_ge(on_sb, NG)
                for ic in range(NC):
                    for b in range(2):
                        turn(ps[0:CH, WV_BANK, ic * C + b * CH:ic * C + (b + 1) * CH],
                             wraw[:, 4 + b, ic * CH:(ic + 1) * CH], ic + b == 0, ic + b == 2)
                for ic in range(NC):
                    last = mm(ps[0:CH, WV_BANK, ic * C:(ic + 1) * C], lora_a[:, 1, ic * CH:(ic + 1) * CH],
                              lora_bt[:, 1, :], start=False, stop=True, skip_group_check=True)
                last.then_inc(wt_ps, 1)

            def out_weights():
                pe.wait_ge(ld_proj, 16)
                pe.wait_ge(ont_sb, 1)
                for b in range(NC):
                    pe.transpose(ps[:, WP_BANK, b * CH:(b + 1) * CH], wpraw[:, b, 0:P], ident[0:CH, 0:CH])
                    last = pe.transpose(ps[0:C - P, WP_BANK, C + b * CH:C + (b + 1) * CH], wpraw[:, b, P:C],
                                        ident[0:CH, 0:CH])
                last.then_inc(wpt_ps, 1)

            for l in range(LAYERS):
                if l == 1:
                    v_weights()
                group_means(l)
                if l == 0:
                    keep_busy(0, 5)
                else:
                    out_weights()
                group_variance(l)
                if l == 0:
                    relative_tables()
                keep_busy(l, BUSY_BEFORE_QK[l])
                pe.wait_ge(xn_sb, 2 * l + 1)
                if l == 0:
                    pe.wait_ge(made_xones, 2)
                    pe.wait_ge(ld_wqk, 64)
                else:
                    pe.wait_ge(ld_b1, 32)
                    pe.wait_ge(wt_sb, 2)
                for ic, rows in enumerate((CH + 1, CH)):
                    if ic == 1:
                        pe.wait_ge(xn_sb, 2 * l + 2)
                    for m in range(3):
                        last = mm(ps[:, m, 0:T], wqk[l][0:rows, ic, m * P:(m + 1) * P], xn[0:rows, ic, :],
                                  start=(ic == 0), stop=(ic == 1))
                        if ic == 1:
                            last.then_inc(qk_ps, 1)
                if l == 0:
                    pe.wait_ge(ld_wv, 32)
                    pe.wait_ge(rello_sb, LAYERS)
                else:
                    pe.wait_ge(wv_sb, 1)
                for t in range(TT):
                    mm(ps[:, V_BANK, t * C:(t + 1) * C], xn[:, 0, t * P:(t + 1) * P], wvv[l][:, 0, :],
                       start=True, stop=False)
                    last = mm(ps[:, V_BANK, t * C:(t + 1) * C], xn[0:CH, 1, t * P:(t + 1) * P],
                              wvv[l][0:CH, 1, :], start=False, stop=True)
                last.then_inc(v_ps, 1)
                if l == 0:
                    pe.wait_ge(tab_sb, 4)
                else:
                    pe.wait_ge(wpt_sb, 2)
                pe.wait_ge(z_lo, 6 * l + NG)
                for which in range(2):
                    for i in range(HW):
                        if which == 0:
                            moving = zq[:, :, i * HW:(i + 1) * HW]
                        else:
                            moving = zq[:, :, :].rearrange("p g (h w) -> p g h w", w=HW)[:, :, :, i]
                        b, c = REL_BANK + 2 * which + i // 8, (i % 8) * NG * HW
                        for part in range(2):
                            last = mm(ps[0:64, b, c:c + NG * HW],
                                      table[l][:, part, which, HW - 1 - i:2 * HW - 1 - i, :].rearrange(
                                          "p r j -> p (r j)"), moving, start=(part == 0), stop=(part == 1))
                        if i % 8 == 7:
                            last.then_inc(rel_ps, 1)
                    for p in ((0, 1, 2), (3, 4, 5))[which]:
                        if p == 0:
                            pe.wait_ge(made_pick, 2)
                            pe.wait_ge(z_lo, 6 * l + 6)
                            pe.wait_ge(v_sb, l + 1)
                        if p >= 4:
                            keys_out(l, p - 4)
                        for a in range(2):
                            h = 2 * p + a
                            last = mm(ps[0:64, K_BANK[p], a * T:(a + 1) * T], pick_k[:, h % G4, :],
                                      zk[:, h // G4, :], start=True, stop=True)
                        last.then_inc(ksel_ps, 1)
                pe.wait_ge(pick_zero, 4)
                pe.wait_ge(made_pick, 6)
                query_rows(l, 0)
                query_rows(l, 1)
                relative_rows(l, 0)
                relative_rows(l, 1)
                query_select(l, 2)
                scores(l, 0)
                query_select(l, 3)
                query_select(l, 4)
                scores_t(l, 0)
                scores(l, 1)
                turn_max(l, 0)
                query_select(l, 5)
                add_max(l, 0)
                scores(l, 2)
                turn_max(l, 1)
                for p in range(PAIRS):
                    if p + 1 < PAIRS:
                        scores_t(l, p + 1)
                    if p + 3 < PAIRS:
                        scores(l, p + 3)
                    if p + 2 < PAIRS:
                        turn_max(l, p + 2)
                    if p + 1 < PAIRS:
                        add_max(l, p + 1)
                    if p in (2, 4):
                        probs_v(l, p // 2 - 1)
                    if p == 5:
                        probs_v(l, 2)
                    if p in (3, 5):
                        turn_out(l, (p - 3) // 2)
                    if l == 0:
                        if p == 3:
                            lora_columns()
                        if p >= 4:
                            qk_weights(p - 4)
                residual(l)
                probs_v(l, 3)
                turn_on(l, 0)
                turn_out(l, 2)
                if l == 0:
                    pe.wait_ge(ld_wo, 48)
                else:
                    pe.wait_ge(ld_bproj, 16)
                    pe.wait_ge(wpt_sb, 2)
                pe.wait_ge(ont_sb, 2 * l + 1)
                for m in range(2):
                    output_product(l, 0, m)
                turn_on(l, 1)
                pe.wait_ge(ont_sb, 2 * l + 2)
                for m in range(2):
                    output_product(l, 1, m).then_inc(y_ps, 1)


_INS = ["x", "L0_conv_wq", "L0_conv_bq", "L0_conv_wk", "L0_conv_bk", "L0_conv_wv", "L0_conv_bv", "L0_conv_wo",
        "L0_conv_bo", "L0_conv_rel_pos_h", "L0_conv_rel_pos_w", "L1_conv_W_qkv", "L1_conv_b_qkv", "L1_conv_A_q",
        "L1_conv_B_q", "L1_conv_A_v", "L1_conv_B_v", "L1_conv_rel_h", "L1_conv_rel_w", "L1_conv_W_proj",
        "L1_conv_b_proj"]


def kernel(**inputs):
    import numpy as _np
    import concourse.bacc as _bacc
    from concourse import mybir as _mybir
    from concourse.bass_utils import run_bass_kernel_spmd as _run

    nc = _bacc.Bacc("TRN2", target_bir_lowering=False, num_devices=1)
    arrays, args = {}, []
    for name in _INS:
        a = _np.ascontiguousarray(inputs[name])
        arrays[f"in_{name}_dram"] = a
        args.append(nc.dram_tensor(f"in_{name}_dram", a.shape, _mybir.dt.from_np(a.dtype), kind="ExternalInput").ap())
    args.append(nc.dram_tensor("out_0_dram", (1, HW, HW, C), F32, kind="ExternalOutput").ap())
    attention_layers(nc, *args)
    r = _run(nc, [arrays], core_ids=[0])
    return r.results[0]["out_0_dram"]
```

```python
from contextlib import ExitStack

import concourse.bass as bass
from concourse import mybir

F32 = mybir.dt.float32
F32R = mybir.dt.float32r
ALU = mybir.AluOpType
ACT = mybir.ActivationFunctionType
AX = mybir.AxisListType

LAYERS = 2
P = 128
HW = 16
T = HW * HW
TT = T // P
C = 192
CH = 96
NC = C // CH
NH = 12
D = C // NH
G4 = 4
NG = NH // G4
PAIRS = NH // 2
GROUP = C // 32
R = 2 * HW - 1
RANK = 4
EPS = 1e-5
SCALE = [float(D) ** 0.5, float(D) ** -0.5]
LORA_SCALE = 1.0 / RANK
VW = 32


def attention_layers(nc, x, w_in0, w_out0, w_in1, w_out1, lora, rel, out):
    ctx = ExitStack()
    with ctx:
        def sb(name, shape, dt=F32):
            return ctx.enter_context(nc.sbuf_tensor(name, shape, dt))

        def sem(name):
            return ctx.enter_context(nc.semaphore(name))

        ident = sb("ident", [P, P])
        ident_r = sb("ident_r", [P, P], F32R)
        busy = sb("busy", [P, P], mybir.dt.bfloat16)
        gavg = sb("gavg", [CH, CH])
        gdev = sb("gdev", [CH, CH])
        warm = sb("warm", [1, 1])
        pow_exp = sb("pow_exp", [CH, NC])
        onehot = sb("onehot", [P, HW, HW])
        head_mask = sb("head_mask", [P, G4])
        pick_q = sb("pick_q", [P, G4, 64], F32R)
        pick_k = sb("pick_k", [P, G4, 64], F32R)
        pick_rh = sb("pick_rh", [P, G4, 64], F32R)
        pick_rl = sb("pick_rl", [P, G4, 64], F32R)
        ones4_raw = sb("ones4_raw", [4, 2, P])
        ones4 = sb("ones4", [4, 2, P], F32R)
        win = [sb(f"win{l}", [CH + 1, NC, 3 * C]) for l in range(LAYERS)]
        wout = [sb(f"wout{l}", [P, 2, C]) for l in range(LAYERS)]
        lora_ab = sb("lora_ab", [RANK, 4, C])
        rel_raw = sb("rel_raw", [P, LAYERS, 2 * R])
        rel_hi = sb("rel_hi", [P, LAYERS, 2 * R], F32R)
        rel_lo = sb("rel_lo", [P, LAYERS, 2 * R], F32R)
        table = [sb(f"table{l}", [P, 2, 2, R, G4], F32R) for l in range(LAYERS)]
        xt = [sb(f"xt{l}", [CH, NC, T]) for l in range(LAYERS)]
        stats = sb("stats", [CH, LAYERS, NC, 6])
        mv = sb("mv", [CH, LAYERS, NC, 2])
        gmean = sb("gmean", [CH, LAYERS, NC])
        ev = sb("ev", [CH, LAYERS, NC])
        vare = sb("vare", [CH, LAYERS, NC])
        rstd = sb("rstd", [CH, LAYERS, NC])
        xn = sb("xn", [CH + 1, NC, T])
        zq = sb("zq", [P, NG, T], F32R)
        zk = sb("zk", [P, NG, T], F32R)
        va = sb("va", [P, TT, NH, VW])
        rr_hi = sb("rr_hi", [P, NG, T], F32R)
        rr_lo = sb("rr_lo", [P, NG, T], F32R)
        qs = sb("qs", [P, NH, T], F32R)
        ks = sb("ks", [P, NH, T], F32R)
        nm = sb("nm", [P, PAIRS, 2, TT])
        nmhl = sb("nmhl", [P, PAIRS, TT, 2, 2], F32R)
        nmt = sb("nmt", [4, PAIRS, T], F32R)
        pt = sb("pt", [P, PAIRS, 2, TT, T])
        ot = sb("ot", [P, NG, T])
        rinv = sb("rinv", [P, NG, TT, G4])
        on = sb("on", [P, TT, C])
        ont = sb("ont", [P, 2, T])
        res = sb("res", [P, TT, C])

        ps = ctx.enter_context(nc.psum_tensor("ps", [P, 8, 512], F32))

        ld_x, ld_rel, ld_lora, stored = (sem(n) for n in ("ld_x", "ld_rel", "ld_lora", "stored"))
        ld_win = [sem(f"ld_win{l}") for l in range(LAYERS)]
        ld_wout = [sem(f"ld_wout{l}") for l in range(LAYERS)]
        zeroed, made_ident, made_gavg, made_ones4, made_ones, made_va = (sem(n) for n in (
            "zeroed", "made_ident", "made_gavg", "made_ones4", "made_ones", "made_va"))
        made_gdev, made_mask, made_pick = (sem(n) for n in ("made_gdev", "made_mask", "made_pick"))
        pick_zero, made_keys, made_ident_r, made_busy = (sem(n) for n in (
            "pick_zero", "made_keys", "made_ident_r", "made_busy"))
        (gn_ps, qk_ps, v_ps, rel_ps, k_ps, q_ps, r_ps, s_ps, st_ps, nmt_ps, o_ps, oq_ps, ont_ps,
         y_ps, lora_ps) = (sem(n) for n in (
            "gn_ps", "qk_ps", "v_ps", "rel_ps", "k_ps", "q_ps", "r_ps", "s_ps", "st_ps", "nmt_ps",
            "o_ps", "oq_ps", "ont_ps", "y_ps", "lora_ps"))
        (warmed, xt_sb, relhi_sb, z_hi, rr_hi_sb, moved_act, nmt_sb, p_sb, ont_sb,
         ot_act, res_act) = (sem(n) for n in (
            "warmed", "xt_sb", "relhi_sb", "z_hi", "rr_hi_sb", "moved_act", "nmt_sb", "p_sb",
            "ont_sb", "ot_act", "res_act"))
        (rello_sb, tab_sb, bn, var_sb, ev_sb, mean_sb, xn_sb, z_lo, v_sb, rr_lo_sb, moved_dve,
         max_sb, nm_hi, nm_lo, ot_sb, ri_sb, on_sb, wl_sb, res_dve) = (sem(n) for n in (
            "rello_sb", "tab_sb", "bn", "var_sb", "ev_sb", "mean_sb", "xn_sb", "z_lo", "v_sb",
            "rr_lo_sb", "moved_dve", "max_sb", "nm_hi", "nm_lo", "ot_sb", "ri_sb", "on_sb",
            "wl_sb", "res_dve"))
        rstd_sb = sem("rstd_sb")

        X_BANK = [3, 4]
        GN_BANK, VAR_BANK = 6, [7, 2]
        V_BANK = [3, 0]
        REL_BANK = 4
        K_BANK, Q_BANK, R_BANK = [0, 1, 2], [3, 5, 2], [4, 6, 7]
        S_BANK = [0, 1]
        ST_BANK = [3, 5]
        O_BANK, NM_BANK = [2, 2, 1], 7
        ONT_BANK = [7, 2]
        Y_BANK = 3
        LORA_BANK = [0, 7]
        ACT_MOVES = [("k", 0, 0), ("k", 1, 0), ("k", 1, 1), ("k", 2, 0), ("k", 2, 1),
                     ("q", 0, 0), ("r", 0, 0), ("q", 1, 0), ("q", 1, 1), ("r", 1, 0), ("r", 1, 1),
                     ("r", 2, 0), ("r", 2, 1), ("q", 2, 0), ("q", 2, 1)]
        DVE_MOVES = [("k", 0, 1), ("q", 0, 1), ("r", 0, 1)]
        BUSY_WITH_MAXIMA = [8, 5]
        BUSY_AT_START = 33
        BUSY_BEFORE_MEANS, BUSY_BEFORE_VARIANCE, BUSY_BEFORE_QK = [0, 5], [8, 9], [17, 14]
        ON_ROWS = [P, C - P]

        out_tokens = out.rearrange("b h w c -> (b h w) c").rearrange("(t p) c -> p t c", p=P)

        block = ctx.enter_context(nc.Block())

        @block.sync
        def _(sp):
            sp.dma_start(xt[0][:, :, :], x.rearrange("(k p) t -> p k t", p=CH)).then_inc(ld_x, 16)
            sp.dma_start(rel_raw[:, :, :], rel).then_inc(ld_rel, 16)
            for l, (w_in, w_out) in enumerate(((w_in0, w_out0), (w_in1, w_out1))):
                sp.dma_start(win[l][:, 0, :], w_in[0:CH + 1, :]).then_inc(ld_win[l], 16)
                sp.dma_start(win[l][0:CH, 1, :], w_in[CH + 1:C + 1, :]).then_inc(ld_win[l], 16)
                if l == 0:
                    sp.dma_start(lora_ab[:, :, :], lora).then_inc(ld_lora, 16)
                sp.dma_start(wout[l][:, 0, :], w_out[0:P, :]).then_inc(ld_wout[l], 16)
                sp.dma_start(wout[l][0:C - P + 1, 1, :], w_out[P:C + 1, :]).then_inc(ld_wout[l], 16)
            sp.wait_ge(res_act, 1)
            sp.wait_ge(res_dve, 1)
            sp.dma_start(out_tokens, res[:, :, :]).then_inc(stored, 16)
            sp.wait_ge(stored, 16)

        def rel_src(which, half):
            v = ps[0:64, REL_BANK + 2 * which + half, 0:8 * NG * HW]
            if which == 0:
                return v.rearrange("p (h g w) -> p g h w", g=NG, w=HW)
            return v.rearrange("p (w g h) -> p g h w", g=NG, h=HW)

        def rel_dst(tile, which, half):
            v = tile[64 * which:64 * which + 64, :, :].rearrange("p g (h w) -> p g h w", w=HW)
            return v[:, :, 8 * half:8 * half + 8, :] if which == 0 else v[:, :, :, 8 * half:8 * half + 8]

        def chunk_rows(which, g):
            m = 64 * (g + NG * which)
            return ps[m % P:m % P + 64, m // P, 0:T]

        def move_args(l, move):
            kind, g, odd = move
            bank, tile, r, done = {"k": (K_BANK, ks, 0, k_ps), "q": (Q_BANK, qs, 0, q_ps),
                                   "r": (R_BANK, qs, 64, r_ps)}[kind]
            return (tile[r:r + 64, G4 * g + odd:G4 * g + odd + 3:2, :],
                    ps[64 * odd:64 * odd + 64, bank[g], :].rearrange("p (u t) -> p u t", t=T),
                    done, NG * l + g + 1)

        @block.gpsimd
        def _(pool):
            def inverse_deviation(l):
                pool.wait_ge(var_sb, l + 1)
                pool.tensor_tensor(rstd[:, l, :], vare[:, l, :], pow_exp[:, :],
                                   ALU.pow).then_inc(rstd_sb, 1)

            pool.memset(ident[:, :], 0.0).then_inc(zeroed, 1)
            pool.wait_ge(zeroed, 1)
            pool.affine_select(out=ident[:, :], in_=ident[:, :], compare_op=ALU.not_equal, fill=1.0,
                               base=0, pattern=[[-1, P]], channel_multiplier=1).then_inc(made_ident, 1)
            pool.memset(gavg[:, :], 1.0 / GROUP).then_inc(zeroed, 1)
            pool.wait_ge(zeroed, 2)
            gv = gavg[:, :].rearrange("p (g k) -> p g k", k=GROUP)
            pool.affine_select(out=gv, in_=gv, compare_op=ALU.is_ge, fill=0.0, base=0,
                               pattern=[[-GROUP, CH // GROUP], [0, GROUP]],
                               channel_multiplier=1).then_inc(zeroed, 1)
            pool.wait_ge(zeroed, 3)
            pool.affine_select(out=gv, in_=gv, compare_op=ALU.is_ge, fill=0.0, base=GROUP - 1,
                               pattern=[[GROUP, CH // GROUP], [0, GROUP]],
                               channel_multiplier=-1).then_inc(made_gavg, 1)
            pool.memset(pow_exp[:, :], -0.5).then_inc(zeroed, 1)
            pool.memset(onehot[:, :, :], 0.0).then_inc(zeroed, 1)
            for n, steps in enumerate(([-1, 0], [0, -1], [-1, 0], [0, -1])):
                pool.wait_ge(zeroed, 5 + n)
                pool.affine_select(out=onehot[:, :, :], in_=onehot[:, :, :], compare_op=ALU.not_equal,
                                   fill=1.0, base=-(64 + D * n), pattern=[[s_, HW] for s_ in steps],
                                   channel_multiplier=1).then_inc(zeroed, 1)
            inverse_deviation(0)
            pool.memset(va[:, :, :, D:VW], 0.0).then_inc(zeroed, 1)
            pool.memset(ones4_raw[:, :, :], 1.0).then_inc(zeroed, 1)
            pool.wait_ge(zeroed, 11)
            pool.memset(va[:, :, :, D:D + 1], 1.0).then_inc(made_va, 1)
            pool.affine_select(out=ones4_raw[:, :, :], in_=ones4_raw[:, :, :],
                               compare_op=ALU.is_ge, fill=0.0, base=0, pattern=[[-2, 2], [0, P]],
                               channel_multiplier=1).then_inc(zeroed, 1)
            pool.wait_ge(zeroed, 12)
            pool.affine_select(out=ones4[:, :, :], in_=ones4_raw[:, :, :],
                               compare_op=ALU.is_ge, fill=0.0, base=1, pattern=[[2, 2], [0, P]],
                               channel_multiplier=-1).then_inc(made_ones4, 1)
            inverse_deviation(1)

        @block.scalar
        def _(act):
            def copy(dst, src, scale=1.0):
                return act.activation(dst, src, ACT.Copy, scale=scale)

            def layer_input():
                for ic in range(NC):
                    act.wait_ge(bn, 4 + ic + 1)
                    copy(xt[1][:, ic, :], ps[0:CH, X_BANK[ic], 0:T]).then_inc(xt_sb, 1)

            act.activation(warm[:, :], nc.const_aps.scalar_like(0.0, warm[:, :]), ACT.Exp).then_inc(warmed, 1)
            act.wait_ge(made_ident, 1)
            by_head = ident[:, :].rearrange("p (s j c) -> p j s c", s=2, j=G4)
            by_pos = ident[:, :].rearrange("p (k j) -> p j k", j=G4)
            copy(ident_r[:, :], ident[:, :]).then_inc(made_ident_r, 1)
            for n in range(2):
                copy(pick_k[:, :, :].rearrange("p j (s r c) -> p r j s c", s=2, r=2)[:, n],
                     by_head).then_inc(made_pick, 1)
            act.wait_ge(ld_rel, 16)
            for l in range(LAYERS):
                copy(rel_hi[:, l, :], rel_raw[:, l, :], scale=1.0 / SCALE[l]).then_inc(relhi_sb, 1)
            for n in range(2):
                copy(pick_q[:, :, :].rearrange("p j (r s c) -> p r j s c", s=2, r=2)[:, n],
                     by_head).then_inc(made_pick, 1)
            copy(pick_rh[:, :, 0:32], by_pos).then_inc(made_pick, 1)
            copy(pick_rl[:, :, 32:64], by_pos).then_inc(made_pick, 1)

            def key_onehots(n):
                act.wait_ge(zeroed, 9)
                copy(ks[64:P, 3 * n:3 * n + 3, :], onehot[64:P, :, :].rearrange("p a b -> p (a b)")
                     .unsqueeze(1).to_broadcast([64, 3, T])).then_inc(made_keys, 1)

            def move(l, n):
                dst, src, done, count = move_args(l, ACT_MOVES[n])
                act.wait_ge(done, count)
                copy(dst, src).then_inc(moved_act, 1)

            def max_rows(l, p):
                act.wait_ge(nmt_ps, PAIRS * l + p + 1)
                copy(nmt[:, p, :], ps[0:4, NM_BANK, 0:T]).then_inc(nmt_sb, 1)

            def probabilities(l, p):
                act.wait_ge(st_ps, PAIRS * l + p + 1)
                act.activation(pt[:, p, :, :, :].rearrange("p a k t -> p a (k t)"),
                               ps[:, ST_BANK[p % 2]:ST_BANK[p % 2] + 2, :], ACT.Exp,
                               scale=SCALE[l]).then_inc(p_sb, 1)

            for l in range(LAYERS):
                if l == 0:
                    for n in range(3):
                        key_onehots(n)
                else:
                    layer_input()
                for which in range(2):
                    for g in range(NG):
                        act.wait_ge(qk_ps, 3 * l + (64 * (g + NG * which)) // P + 1)
                        copy((zq, zk)[which][0:64, g, :], chunk_rows(which, g)).then_inc(z_hi, 1)
                    if l == 0 and which == 1:
                        key_onehots(3)
                for which in range(2):
                    for half in range(2):
                        act.wait_ge(rel_ps, 4 * l + 2 * which + half + 1)
                        copy(rel_dst(rr_hi, which, half), rel_src(which, half)).then_inc(rr_hi_sb, 1)
                    if which == 0:
                        for n in range(3):
                            move(l, n)
                for n in range(3, 13):
                    move(l, n)
                max_rows(l, 0)
                for n in range(13, 15):
                    move(l, n)
                for p in range(PAIRS):
                    probabilities(l, p)
                    if p == 0:
                        max_rows(l, 1)
                    if p + 2 < PAIRS:
                        max_rows(l, p + 2)
                for n, r0 in ((2, 0), (3, 64)):
                    act.wait_ge(o_ps, 4 * l + n + 1)
                    copy(ot[r0:r0 + 64, 2, :], ps[r0:r0 + 64, O_BANK[2], 0:T]).then_inc(ot_act, 1)
                for kc in range(2):
                    act.wait_ge(ont_ps, 2 * l + kc + 1)
                    copy(ont[0:ON_ROWS[kc], kc, :],
                         ps[0:ON_ROWS[kc], ONT_BANK[kc], 0:T]).then_inc(ont_sb, 1)
            act.wait_ge(y_ps, NC + 1)
            copy(res[:, 0, :], ps[:, Y_BANK, 0:C]).then_inc(res_act, 1)

        @block.vector
        def _(dve):
            dve.memset(busy[:, :], 0.0).then_inc(made_busy, 1)
            dve.memset(xn[CH:CH + 1, 0, :], 1.0).then_inc(made_ones, 1)
            dve.memset(ont[C - P:C - P + 1, 1, :], 1.0).then_inc(made_ones, 1)
            dve.memset(pick_rh[:, :, 32:64].bitcast(F32), 0.0).then_inc(pick_zero, 1)
            dve.memset(pick_rl[:, :, 0:32].bitcast(F32), 0.0).then_inc(pick_zero, 1)
            dve.wait_ge(made_ident, 1)
            dve.tensor_reduce(head_mask[:, :], ident[:, :].rearrange("p (s j c) -> p j s c", s=2, j=G4),
                              AX.XY, ALU.add).then_inc(made_mask, 1)
            dve.wait_ge(made_gavg, 1)
            dve.tensor_tensor(gdev[:, :], ident[0:CH, 0:CH], gavg[:, :], ALU.subtract).then_inc(made_gdev, 1)

            def move(l, n):
                dst, src, done, count = move_args(l, DVE_MOVES[n])
                dve.wait_ge(done, count)
                dve.tensor_copy(dst, src).then_inc(moved_dve, 1)

            def normalise(l, g):
                dve.wait_ge(oq_ps, NG * l + g + 1)
                q = ps[:, O_BANK[g], T:2 * T].rearrange("p (t j d) -> p t j d", t=TT, j=G4)
                dve.reciprocal(rinv[:, g, :, :], q[:, :, :, D]).then_inc(ri_sb, 1)
                dve.wait_ge(ri_sb, NG * l + g + 1)
                dve.tensor_tensor(
                    on[:, :, 64 * g:64 * g + 64].rearrange("p t (j d) -> p t j d", d=D), q[:, :, :, 0:D],
                    rinv[:, g, :, :].unsqueeze(3).to_broadcast([P, TT, G4, D]), ALU.mult).then_inc(on_sb, 1)

            def maxima(l, p):
                for a in range(2):
                    dve.wait_ge(s_ps, NH * l + 2 * p + a + 1)
                    dve.tensor_reduce(nm[:, p, a, :], ps[:, S_BANK[a], :].rearrange("p (t k) -> p t k", k=T),
                                      AX.X, ALU.max, negate=True).then_inc(max_sb, 1)
                by_tile = nm[:, p, :, :].rearrange("p a t -> p t a")
                dve.wait_ge(max_sb, NH * l + 2 * p + 2)
                dve.tensor_copy(nmhl[:, p, :, :, 0], by_tile).then_inc(nm_hi, 1)
                dve.wait_ge(nm_hi, PAIRS * l + p + 1)
                dve.tensor_tensor(nmhl[:, p, :, :, 1], by_tile, nmhl[:, p, :, :, 0].bitcast(F32),
                                  ALU.subtract).then_inc(nm_lo, 1)

            def out_columns(l, g):
                dve.wait_ge(o_ps, 4 * l + g + 1)
                dve.tensor_copy(ot[:, g, :], ps[:, O_BANK[g], 0:T]).then_inc(ot_sb, 1)

            def values(l, t):
                dve.wait_ge(v_ps, TT * l + t + 1)
                dve.tensor_copy(va[:, t, :, 0:D], ps[:, V_BANK[t], 0:C].rearrange("p (h d) -> p h d", d=D)
                                ).then_inc(v_sb, 1)

            def lora(s):
                dve.wait_ge(ld_win[1], 32)
                dve.wait_ge(lora_ps, s + 1)
                cols = win[1][0:CH, :, 2 * s * C:(2 * s + 1) * C]
                dve.scalar_tensor_tensor(
                    out=cols, in0=ps[0:CH, LORA_BANK[s], 0:2 * C].rearrange("p (k n) -> p k n", k=NC),
                    scalar=LORA_SCALE, in1=cols, op0=ALU.mult, op1=ALU.add).then_inc(wl_sb, 1)

            for l in range(LAYERS):
                for ic in range(NC):
                    if l == 0:
                        dve.wait_ge(ld_x, 16)
                        source = xt[0][:, ic, :]
                    else:
                        dve.wait_ge(y_ps, ic + 1)
                        source = ps[0:CH, X_BANK[ic], 0:T]
                    dve.bn_stats(stats[:, l, ic, :], source).then_inc(bn, 1)
                for ic in range(NC):
                    dve.wait_ge(bn, 4 * l + ic + 1)
                    dve.bn_aggr(mv[:, l, ic, :], stats[:, l, ic, :]).then_inc(bn, 1)
                dve.wait_ge(bn, 4 * l + 4)
                dve.wait_ge(gn_ps, 2 * l + 1)
                for ic in range(NC):
                    dev = ps[0:CH, GN_BANK, 2 + ic:3 + ic]
                    dve.scalar_tensor_tensor(out=ev[:, l, ic:ic + 1], in0=dev, scalar=dev,
                                             in1=mv[:, l, ic, 1:2],
                                             op0=ALU.mult, op1=ALU.add).then_inc(ev_sb, 1)
                dve.tensor_copy(gmean[:, l, :], ps[0:CH, GN_BANK, 0:2]).then_inc(mean_sb, 1)
                dve.wait_ge(gn_ps, 2 * l + 2)
                dve.tensor_scalar(vare[:, l, :], ps[0:CH, VAR_BANK[l], 0:2], EPS, None,
                                  ALU.add).then_inc(var_sb, 1)
                dve.wait_ge(mean_sb, l + 1)
                if l == 1:
                    lora(0)
                    dve.wait_ge(xt_sb, NC)
                dve.wait_ge(rstd_sb, l + 1)
                for ic in range(NC):
                    dve.tensor_scalar(xn[0:CH, ic, :], xt[l][:, ic, :], gmean[:, l, ic:ic + 1],
                                      rstd[:, l, ic:ic + 1], ALU.subtract, ALU.mult).then_inc(xn_sb, 1)
                if l == 1:
                    lora(1)
                if l == 0:
                    dve.wait_ge(relhi_sb, LAYERS)
                    for k in range(LAYERS):
                        dve.scalar_tensor_tensor(out=rel_lo[:, k, :], in0=rel_raw[:, k, :],
                                                 scalar=1.0 / SCALE[k], in1=rel_hi[:, k, :].bitcast(F32),
                                                 op0=ALU.mult, op1=ALU.subtract).then_inc(rello_sb, 1)
                    dve.wait_ge(made_mask, 1)
                    for k in range(LAYERS):
                        dve.wait_ge(rello_sb, k + 1)
                        for part, half in enumerate((rel_hi, rel_lo)):
                            dve.tensor_tensor(
                                table[k][:, part, :, :, :].rearrange("p s r j -> p (s r) j"),
                                half[:, k, :].bitcast(F32).unsqueeze(2).to_broadcast([P, 2 * R, G4]),
                                head_mask[:, :].unsqueeze(1).to_broadcast([P, 2 * R, G4]),
                                ALU.mult).then_inc(tab_sb, 1)
                for which in range(2):
                    for g in range(NG):
                        z = (zq, zk)[which]
                        dve.wait_ge(z_hi, 6 * l + NG * which + g + 1)
                        dve.tensor_tensor(z[64:P, g, :], chunk_rows(which, g), z[0:64, g, :].bitcast(F32),
                                          ALU.subtract).then_inc(z_lo, 1)
                values(l, 0)
                for which in range(2):
                    for half in range(2):
                        n = 4 * l + 2 * which + half + 1
                        dve.wait_ge(rr_hi_sb, n)
                        dve.tensor_tensor(rel_dst(rr_lo, which, half), rel_src(which, half),
                                          rel_dst(rr_hi, which, half).bitcast(F32),
                                          ALU.subtract).then_inc(rr_lo_sb, 1)
                    if which == 0:
                        move(l, 0)
                move(l, 1)
                values(l, 1)
                move(l, 2)
                for p in range(PAIRS):
                    maxima(l, p)
                out_columns(l, 0)
                normalise(l, 0)
                out_columns(l, 1)
                normalise(l, 1)
                normalise(l, 2)
            dve.wait_ge(y_ps, NC + 2)
            dve.tensor_copy(res[:, 1, :], ps[:, Y_BANK + 1, 0:C]).then_inc(res_dve, 1)

        @block.tensor
        def _(pe):
            mm = pe.matmul

            def keep_busy(n, bank=5):
                for _ in range(n):
                    mm(ps[:, bank, 0:P], busy[:, :], busy[:, :], start=True, stop=True)

            pe.wait_ge(made_busy, 1)
            keep_busy(BUSY_AT_START)

            def group_means(l):
                pe.wait_ge(bn, 4 * l + 4)
                pe.wait_ge(made_gavg, 1)
                pe.wait_ge(made_gdev, 1)
                mm(ps[0:CH, GN_BANK, 0:2], gavg[:, :], mv[:, l, :, 0], start=True, stop=True)
                mm(ps[0:CH, GN_BANK, 2:4], gdev[:, :], mv[:, l, :, 0], start=True,
                   stop=True).then_inc(gn_ps, 1)

            def group_variance(l):
                pe.wait_ge(ev_sb, 2 * l + 2)
                mm(ps[0:CH, VAR_BANK[l], 0:2], gavg[:, :], ev[:, l, :], start=True,
                   stop=True).then_inc(gn_ps, 1)

            def moved(l, *moves):
                for engine_moves, signal in ((ACT_MOVES, moved_act), (DVE_MOVES, moved_dve)):
                    last = max((engine_moves.index(m) + 1 for m in moves if m in engine_moves), default=0)
                    if last:
                        pe.wait_ge(signal, len(engine_moves) * l + last)

            def both(kind, g):
                return (kind, g, 0), (kind, g, 1)

            def key_rows(l, g):
                if g == 0:
                    pe.wait_ge(made_pick, 2)
                    pe.wait_ge(z_lo, 6 * l + 6)
                for u in range(2):
                    last = mm(ps[:, K_BANK[g], u * T:(u + 1) * T],
                              pick_k[:, 2 * u:2 * u + 2, :].rearrange("p j n -> p (j n)"), zk[:, g, :],
                              start=True, stop=True)
                last.then_inc(k_ps, 1)

            def query_rows(l, g):
                if g == 0:
                    pe.wait_ge(made_pick, 6)
                    pe.wait_ge(v_sb, TT * l + 1)
                elif g == 1:
                    pe.wait_ge(rr_lo_sb, 4 * l + 4)
                else:
                    moved(l, *both("k", 2))
                for u in range(2):
                    last = mm(ps[:, Q_BANK[g], u * T:(u + 1) * T],
                              pick_q[:, 2 * u:2 * u + 2, :].rearrange("p j n -> p (j n)"), zq[:, g, :],
                              start=True, stop=True)
                last.then_inc(q_ps, 1)

            def relative_rows(l, g):
                pe.wait_ge(pick_zero, 2)
                if g > 0:
                    pe.wait_ge(rr_lo_sb, 4 * l + 4)
                else:
                    pe.wait_ge(rr_lo_sb, 4 * l + 1)
                for part, (pick, rr, split) in enumerate(((pick_rh, rr_hi, rr_hi_sb), (pick_rl, rr_lo, rr_lo_sb))):
                    pe.wait_ge(split, 4 * l + 4)
                    for u in range(2):
                        last = mm(ps[:, R_BANK[g], u * T:(u + 1) * T],
                                  pick[:, 2 * u:2 * u + 2, :].rearrange("p j n -> p (j n)"), rr[:, g, :],
                                  start=(part == 0 and u == 0), stop=(part == 1), skip_group_check=True)
                last.then_inc(r_ps, 1)

            def scores(l, p, heads=(0, 1)):
                if p == 0 and 0 in heads:
                    pe.wait_ge(made_keys, 4)
                    moved(l, *(m for g in range(NG) for m in both("k", g)))
                    pe.wait_ge(v_sb, TT * l + 2)
                moved(l, *both("q", p // 2), *both("r", p // 2))
                for a in heads:
                    if p >= 1:
                        pe.wait_ge(max_sb, NH * l + 2 * p + a - 1)
                    for t in range(TT):
                        last = mm(ps[:, S_BANK[a], t * T:(t + 1) * T],
                                  qs[:, 2 * p + a, t * P:(t + 1) * P], ks[:, 2 * p + a, :],
                                  start=True, stop=True)
                    last.then_inc(s_ps, 1)

            def scores_t(l, p):
                if p == 0:
                    moved(l, *both("q", 0), *both("r", 0))
                elif p == 1:
                    moved(l, *both("q", 1), *both("r", 1))
                else:
                    pe.wait_ge(p_sb, PAIRS * l + p - 1)
                for a in range(2):
                    for t in range(TT):
                        mm(ps[:, ST_BANK[p % 2] + a, t * T:(t + 1) * T],
                           ks[:, 2 * p + a, t * P:(t + 1) * P], qs[:, 2 * p + a, :],
                           start=(t == 0), stop=False, skip_group_check=True)

            def turn_max(l, p):
                if p == 0:
                    pe.wait_ge(made_ident_r, 1)
                    moved(l, *both("r", 2))
                else:
                    pe.wait_ge(nmt_sb, PAIRS * l + p)
                pe.wait_ge(nm_lo, PAIRS * l + p + 1)
                for t in range(TT):
                    last = mm(ps[0:4, NM_BANK, t * P:(t + 1) * P],
                              nmhl[:, p, t, :, :].rearrange("p a s -> p (a s)"), ident_r[:, :],
                              start=True, stop=True)
                last.then_inc(nmt_ps, 1)

            def add_max(l, p):
                if l == 0 and p == 0:
                    pe.wait_ge(made_ones4, 1)
                pe.wait_ge(nmt_sb, PAIRS * l + p + 1)
                for a in range(2):
                    for t in range(TT):
                        last = mm(ps[:, ST_BANK[p % 2] + a, t * T:(t + 1) * T], ones4[:, a, :], nmt[:, p, :],
                                  start=False, stop=True, skip_group_check=True)
                last.then_inc(st_ps, 1)

            def probs_v(l, n):
                g, heads = ((0, (0, 1, 2, 3)), (1, (0, 1, 2, 3)), (2, (0, 1)), (2, (2, 3)))[n]
                if n == 0:
                    moved(l, *both("q", 2))
                    pe.wait_ge(v_sb, TT * l + 2)
                    pe.wait_ge(made_va, 1)
                elif n == 1:
                    pe.wait_ge(on_sb, NG * l + 1)
                elif n == 2:
                    pe.wait_ge(max_sb, NH * l + NH)
                pe.wait_ge(p_sb, PAIRS * l + (2, 4, 5, 6)[n])
                for t in range(TT):
                    for j in heads:
                        last = mm(ps[32 * j:32 * j + 32, O_BANK[g], 0:T], va[:, t, G4 * g + j, :],
                                  pt[:, 2 * g + j // 2, j % 2, t, :], start=(t == 0), stop=(t == TT - 1))
                last.then_inc(o_ps, 1)

            def turn_out(l, g):
                if g < 2:
                    pe.wait_ge(ot_sb, 2 * l + g + 1)
                else:
                    pe.wait_ge(ot_act, 2 * l + 2)
                for t in range(TT):
                    last = pe.transpose(ps[:, O_BANK[g], T + t * P:T + (t + 1) * P],
                                        ot[:, g, t * P:(t + 1) * P], ident[:, :])
                last.then_inc(oq_ps, 1)

            def turn_on(l, kc):
                pe.wait_ge(on_sb, NG * l + 2 + kc)
                for t in range(TT):
                    last = pe.transpose(ps[0:ON_ROWS[kc], ONT_BANK[kc], t * P:(t + 1) * P],
                                        on[:, t, kc * P:kc * P + ON_ROWS[kc]], ident[:, :])
                last.then_inc(ont_ps, 1)

            def residual(l, m):
                pe.wait_ge(p_sb, PAIRS * l + PAIRS - 1)
                if l == 0:
                    mm(ps[0:CH, Y_BANK + m, 0:T], ident[0:CH, 0:CH], xt[0][:, m, :], start=True,
                       stop=False, skip_group_check=True)
                else:
                    pe.wait_ge(xt_sb, NC)
                    for ic in range(NC):
                        mm(ps[:, Y_BANK + m, ic * CH:(ic + 1) * CH], xt[1][:, ic, m * P:(m + 1) * P],
                           ident[0:CH, 0:CH], start=(ic == 0), stop=False, is_transpose=True,
                           skip_group_check=True)

            def output_product(l, kc, m):
                k = ON_ROWS[kc] + kc
                if l == 0:
                    return mm(ps[0:CH, Y_BANK + m, 0:T], wout[0][0:k, kc, m * CH:(m + 1) * CH],
                              ont[0:k, kc, :], start=False, stop=(kc == 1), skip_group_check=True)
                return mm(ps[:, Y_BANK + m, 0:C], ont[0:k, kc, m * P:(m + 1) * P],
                          wout[1][0:k, kc, :], start=False, stop=(kc == 1), skip_group_check=True)

            def lora_columns(s):
                pe.wait_ge(ld_lora, 16)
                for ic in range(NC):
                    last = mm(ps[0:CH, LORA_BANK[s], ic * C:(ic + 1) * C],
                              lora_ab[:, s, ic * CH:(ic + 1) * CH], lora_ab[:, 2 + s, :],
                              start=True, stop=True)
                last.then_inc(lora_ps, 1)

            def values(l, t):
                if t == 1:
                    moved(l, *both("k", 0))
                for ic in range(NC):
                    rows = CH + 1 - ic
                    last = mm(ps[:, V_BANK[t], 0:C], xn[0:rows, ic, t * P:(t + 1) * P],
                              win[l][0:rows, ic, 2 * C:3 * C], start=(ic == 0), stop=(ic == 1))
                last.then_inc(v_ps, 1)

            for l in range(LAYERS):
                if l == 1:
                    lora_columns(0)
                keep_busy(BUSY_BEFORE_MEANS[l])
                group_means(l)
                keep_busy(BUSY_BEFORE_VARIANCE[l])
                group_variance(l)
                if l == 1:
                    lora_columns(1)
                keep_busy(BUSY_BEFORE_QK[l])
                pe.wait_ge(xn_sb, 2 * l + 1)
                pe.wait_ge(made_ones, 2)
                pe.wait_ge(ld_win[l], 32)
                if l == 1:
                    pe.wait_ge(wl_sb, 1)
                for ic, m in ((0, 0), (0, 1), (1, 0), (1, 1), (0, 2), (1, 2)):
                    if (ic, m) == (1, 0):
                        pe.wait_ge(xn_sb, 2 * l + 2)
                    rows = CH + 1 - ic
                    last = mm(ps[:, m, 0:T], win[l][0:rows, ic, m * P:(m + 1) * P], xn[0:rows, ic, :],
                              start=(ic == 0), stop=(ic == 1))
                    if ic == 1:
                        last.then_inc(qk_ps, 1)
                if l == 1:
                    pe.wait_ge(wl_sb, 2)
                values(l, 0)
                if l == 0:
                    pe.wait_ge(tab_sb, 4)
                pe.wait_ge(z_lo, 6 * l + NG)
                for which in range(2):
                    for i in range(HW):
                        if which == 0:
                            moving = zq[:, :, i * HW:(i + 1) * HW]
                        else:
                            moving = zq[:, :, :].rearrange("p g (h w) -> p g h w", w=HW)[:, :, :, i]
                        b, c = REL_BANK + 2 * which + i // 8, (i % 8) * NG * HW
                        for part in range(2):
                            last = mm(ps[0:64, b, c:c + NG * HW],
                                      table[l][:, part, which, HW - 1 - i:2 * HW - 1 - i, :].rearrange(
                                          "p r j -> p (r j)"), moving, start=(part == 0), stop=(part == 1))
                        if i % 8 == 7:
                            last.then_inc(rel_ps, 1)
                    if which == 0:
                        key_rows(l, 0)
                        key_rows(l, 1)
                key_rows(l, 2)
                query_rows(l, 0)
                values(l, 1)
                relative_rows(l, 0)
                query_rows(l, 1)
                relative_rows(l, 1)
                relative_rows(l, 2)
                query_rows(l, 2)
                scores(l, 0)
                scores_t(l, 0)
                scores(l, 1)
                scores_t(l, 1)
                turn_max(l, 0)
                scores(l, 2)
                add_max(l, 0)
                turn_max(l, 1)
                moved(l, *both("q", 2))
                keep_busy(BUSY_WITH_MAXIMA[0], bank=O_BANK[0])
                for p in range(PAIRS):
                    if 0 < p and p + 1 < PAIRS:
                        scores_t(l, p + 1)
                    if p + 3 < PAIRS:
                        scores(l, p + 3)
                    if p == 0:
                        keep_busy(BUSY_WITH_MAXIMA[1], bank=O_BANK[0])
                    if p + 2 < PAIRS:
                        turn_max(l, p + 2)
                    if p + 1 < PAIRS:
                        add_max(l, p + 1)
                    if p in (2, 4):
                        probs_v(l, p // 2 - 1)
                    if p == 5:
                        probs_v(l, 2)
                    if p in (3, 5):
                        turn_out(l, (p - 3) // 2)
                probs_v(l, 3)
                residual(l, 0)
                turn_out(l, 2)
                turn_on(l, 0)
                residual(l, 1)
                turn_on(l, 1)
                pe.wait_ge(ld_wout[l], 32)
                pe.wait_ge(ont_sb, 2 * l + 1)
                for m in range(2):
                    output_product(l, 0, m)
                pe.wait_ge(ont_sb, 2 * l + 2)
                for m in range(2):
                    output_product(l, 1, m).then_inc(y_ps, 1)


def kernel(**inputs):
    import numpy as _np
    import concourse.bacc as _bacc
    from concourse import mybir as _mybir
    from concourse.bass_utils import run_bass_kernel_spmd as _run

    nc = _bacc.Bacc("TRN2", target_bir_lowering=False, num_devices=1)
    w = {name: _np.asarray(a) for name, a in inputs.items()}

    def with_bias(row, weights, bias):
        return _np.insert(weights, row, bias, axis=0)

    def columns(rel):
        return _np.tile(rel[::-1].T, (P // D, 1))

    packed = {
        "x": w["x"].reshape(T, C).T,
        "w_in0": with_bias(CH, _np.concatenate([w[f"L0_conv_w{n}"] for n in "qkv"], axis=1),
                           _np.concatenate([w[f"L0_conv_b{n}"] for n in "qkv"])),
        "w_out0": with_bias(C, w["L0_conv_wo"], w["L0_conv_bo"]),
        "w_in1": with_bias(CH, w["L1_conv_W_qkv"].T, w["L1_conv_b_qkv"]),
        "w_out1": with_bias(C, w["L1_conv_W_proj"].T, w["L1_conv_b_proj"]),
        "lora": _np.stack([w["L1_conv_A_q"], w["L1_conv_A_v"], w["L1_conv_B_q"].T, w["L1_conv_B_v"].T], axis=1),
        "rel": _np.concatenate([columns(w[n]) for n in ("L0_conv_rel_pos_h", "L0_conv_rel_pos_w",
                                                        "L1_conv_rel_h", "L1_conv_rel_w")], axis=1)
        .reshape(P, LAYERS, 2 * R),
    }
    arrays, args = {}, []
    for name, a in packed.items():
        a = _np.ascontiguousarray(a)
        arrays[f"in_{name}_dram"] = a
        args.append(nc.dram_tensor(f"in_{name}_dram", a.shape, _mybir.dt.from_np(a.dtype), kind="ExternalInput").ap())
    args.append(nc.dram_tensor("out_0_dram", (1, HW, HW, C), F32, kind="ExternalOutput").ap())
    attention_layers(nc, *args)
    r = _run(nc, [arrays], core_ids=[0])
    return r.results[0]["out_0_dram"]
```
